# Optimizing a Trainium2 kernel written in Bass

```python
import numpy as np
import jax
import jax.numpy as jnp

def _softmax(x, axis=-1):
    return jax.nn.softmax(x, axis=axis)

def _gelu(x):
    return jax.nn.gelu(x, approximate=True)

def _silu(x):
    return jax.nn.silu(x)

def _sigmoid(x):
    return jax.nn.sigmoid(x)

def _layernorm(x, axis=-1, eps=1e-05):
    m = jnp.mean(x, axis=axis, keepdims=True)
    v = jnp.var(x, axis=axis, keepdims=True)
    return (x - m) / jnp.sqrt(v + eps)

def _scatter_add(tgt, idx, src, axis=0):
    return tgt.at[idx].add(src)

def _segment_sum(src, seg, n):
    return jax.ops.segment_sum(src, seg, n)
kernel_name = 'mk_conv_seq_d2_conv_nhwc256_r2_46553b'

def setup_inputs(seed: int=0):
    np.random.seed(seed)
    _w = jnp.asarray

    def _rec_inputs():
        import jax
        import jax.numpy as jnp
        _gk = jax.random.key(seed)
        x = -0.0002091 + 1 * jax.random.normal(jax.random.fold_in(_gk, 1), (32, 56, 56, 128), jnp.float32)
        return x
    x = _rec_inputs()

    def _L0_conv_setup():
        import jax, jax.numpy as jnp
        import numpy as np
        from jax import lax
        EPS = 0.001
        CARDINALITY = 32
        DN = ('NHWC', 'HWIO', 'NHWC')

        def _bn(x, gamma, beta, mean, var):
            return (x - mean) * lax.rsqrt(var + EPS) * gamma + beta
        key = jax.random.key(seed)
        ks = jax.random.split(key, 8)
        B, H, W = (32, 56, 56)
        F = 32
        mid = 2 * F
        cout = 4 * F
        x = jax.random.normal(ks[0], (B, H, W, cout), jnp.float32)
        w1 = jax.random.normal(ks[1], (1, 1, cout, mid), jnp.float32) * 0.05
        w2 = jax.random.normal(ks[2], (3, 3, mid // CARDINALITY, mid), jnp.float32) * 0.05
        w3 = jax.random.normal(ks[3], (1, 1, mid, cout), jnp.float32) * 0.05

        def bn_params(k, c):
            k1, k2, k3, k4 = jax.random.split(k, 4)
            gamma = 1.0 + 0.1 * jax.random.normal(k1, (c,), jnp.float32)
            beta = 0.1 * jax.random.normal(k2, (c,), jnp.float32)
            mean = 0.1 * jax.random.normal(k3, (c,), jnp.float32)
            var = jax.random.uniform(k4, (c,), jnp.float32) + 0.5
            return (gamma, beta, mean, var)
        g1, b1, m1, v1 = bn_params(ks[4], mid)
        g2, b2, m2, v2 = bn_params(ks[5], mid)
        g3, b3, m3, v3 = bn_params(ks[6], cout)
        return dict(x=x, w1=w1, g1=g1, b1=b1, m1=m1, v1=v1, w2=w2, g2=g2, b2=b2, m2=m2, v2=v2, w3=w3, g3=g3, b3=b3, m3=m3, v3=v3)
    _L0_conv_all = _L0_conv_setup()
    _L0_conv_in = {k: v for k, v in _L0_conv_all.items() if k in ('w1', 'g1', 'b1', 'm1', 'v1', 'w2', 'g2', 'b2', 'm2', 'v2', 'w3', 'g3', 'b3', 'm3', 'v3')}
    del _L0_conv_all

    def _L1_conv_setup():
        import jax, jax.numpy as jnp
        import numpy as np
        WS = (7, 7)
        SS = (3, 3)
        NUM_HEADS = 8
        NEG = -1000000000.0

        def _rel_index(ws):
            Wh, Ww = ws
            ch, cw = np.meshgrid(np.arange(Wh), np.arange(Ww), indexing='ij')
            coords = np.stack([ch, cw]).reshape(2, -1)
            rel = coords[:, :, None] - coords[:, None, :]
            rel = rel.transpose(1, 2, 0).astype(np.int64)
            rel[..., 0] += Wh - 1
            rel[..., 1] += Ww - 1
            rel[..., 0] *= 2 * Ww - 1
            return rel.sum(-1)

        def _swin_mask(H, W, ws, ss):
            img = np.zeros((H, W))
            hs = (slice(0, -ws[0]), slice(-ws[0], -ss[0]), slice(-ss[0], None)) if 0 < ss[0] < ws[0] else (slice(None),)
            wsl = (slice(0, -ws[1]), slice(-ws[1], -ss[1]), slice(-ss[1], None)) if 0 < ss[1] < ws[1] else (slice(None),)
            cnt = 0
            for h in hs:
                for w in wsl:
                    img[h, w] = cnt
                    cnt += 1
            m = img.reshape(H // ws[0], ws[0], W // ws[1], ws[1]).transpose(0, 2, 1, 3).reshape(-1, ws[0] * ws[1])
            diff = m[:, None, :] - m[:, :, None]
            return np.where(diff != 0, NEG, 0.0).astype(np.float32)

        def _coords_table(ws, h_times, ws_scalar, ws_scalar2, pow_para):
            Wh, Ww = ws
            ch = jnp.arange(-(Wh - 1), Wh, dtype=jnp.float32) / max(Wh - 1, 1)
            cw = jnp.arange(-(Ww - 1), Ww, dtype=jnp.float32) / max(Ww - 1, 1)
            tab = jnp.stack(jnp.meshgrid(ch, cw, indexing='ij'), axis=-1)
            tab = tab * h_times
            tab = jnp.sign(tab) * jnp.power(jnp.abs(tab) * ws_scalar + 1e-06, pow_para) / ws_scalar2
            return tab.reshape(-1, 2)

        def _ln(x, w, b):
            mu = x.mean(-1, keepdims=True)
            var = x.var(-1, keepdims=True)
            return (x - mu) / jnp.sqrt(var + 1e-05) * w + b
        key = jax.random.key(seed)
        ks = jax.random.split(key, 8)
        B, H, W, C = (32, 56, 56, 128)
        hid = 4 * C
        s = 0.02
        return {'x': jax.random.normal(ks[0], (B, H, W, C), jnp.float32), 'norm1_w': jnp.ones((C,), jnp.float32), 'norm1_b': jnp.zeros((C,), jnp.float32), 'qkv_w': jax.random.normal(ks[1], (3 * C, C), jnp.float32) * s, 'proj_w': jax.random.normal(ks[2], (C, C), jnp.float32) * s, 'proj_b': jnp.zeros((C,), jnp.float32), 'cpb_w1': jax.random.normal(ks[3], (256, 2), jnp.float32) * s, 'cpb_b1': jnp.zeros((256,), jnp.float32), 'cpb_w2': jax.random.normal(ks[4], (NUM_HEADS, 256), jnp.float32) * s, 'h_times': jnp.asarray(2.0, jnp.float32), 'pow_para': jnp.asarray(0.0, jnp.float32), 'ws_scalar': jnp.asarray(1.0, jnp.float32), 'ws_scalar2': jnp.asarray(2.0, jnp.float32), 'norm2_w': jnp.ones((C,), jnp.float32), 'norm2_b': jnp.zeros((C,), jnp.float32), 'fc1_w': jax.random.normal(ks[5], (hid, C), jnp.float32) * s, 'fc1_b': jnp.zeros((hid,), jnp.float32), 'fc2_w': jax.random.normal(ks[6], (C, hid), jnp.float32) * s, 'fc2_b': jnp.zeros((C,), jnp.float32)}
    _L1_conv_all = _L1_conv_setup()
    _L1_conv_in = {k: v for k, v in _L1_conv_all.items() if k in ('norm1_w', 'norm1_b', 'qkv_w', 'proj_w', 'proj_b', 'cpb_w1', 'cpb_b1', 'cpb_w2', 'h_times', 'pow_para', 'ws_scalar', 'ws_scalar2', 'norm2_w', 'norm2_b', 'fc1_w', 'fc1_b', 'fc2_w', 'fc2_b')}
    del _L1_conv_all
    return {'x': x, 'L0_conv_w1': _L0_conv_in['w1'], 'L0_conv_g1': _L0_conv_in['g1'], 'L0_conv_b1': _L0_conv_in['b1'], 'L0_conv_m1': _L0_conv_in['m1'], 'L0_conv_v1': _L0_conv_in['v1'], 'L0_conv_w2': _L0_conv_in['w2'], 'L0_conv_g2': _L0_conv_in['g2'], 'L0_conv_b2': _L0_conv_in['b2'], 'L0_conv_m2': _L0_conv_in['m2'], 'L0_conv_v2': _L0_conv_in['v2'], 'L0_conv_w3': _L0_conv_in['w3'], 'L0_conv_g3': _L0_conv_in['g3'], 'L0_conv_b3': _L0_conv_in['b3'], 'L0_conv_m3': _L0_conv_in['m3'], 'L0_conv_v3': _L0_conv_in['v3'], 'L1_conv_norm1_w': _L1_conv_in['norm1_w'], 'L1_conv_norm1_b': _L1_conv_in['norm1_b'], 'L1_conv_qkv_w': _L1_conv_in['qkv_w'], 'L1_conv_proj_w': _L1_conv_in['proj_w'], 'L1_conv_proj_b': _L1_conv_in['proj_b'], 'L1_conv_cpb_w1': _L1_conv_in['cpb_w1'], 'L1_conv_cpb_b1': _L1_conv_in['cpb_b1'], 'L1_conv_cpb_w2': _L1_conv_in['cpb_w2'], 'L1_conv_h_times': _L1_conv_in['h_times'], 'L1_conv_pow_para': _L1_conv_in['pow_para'], 'L1_conv_ws_scalar': _L1_conv_in['ws_scalar'], 'L1_conv_ws_scalar2': _L1_conv_in['ws_scalar2'], 'L1_conv_norm2_w': _L1_conv_in['norm2_w'], 'L1_conv_norm2_b': _L1_conv_in['norm2_b'], 'L1_conv_fc1_w': _L1_conv_in['fc1_w'], 'L1_conv_fc1_b': _L1_conv_in['fc1_b'], 'L1_conv_fc2_w': _L1_conv_in['fc2_w'], 'L1_conv_fc2_b': _L1_conv_in['fc2_b']}

def reference(x, L0_conv_w1, L0_conv_g1, L0_conv_b1, L0_conv_m1, L0_conv_v1, L0_conv_w2, L0_conv_g2, L0_conv_b2, L0_conv_m2, L0_conv_v2, L0_conv_w3, L0_conv_g3, L0_conv_b3, L0_conv_m3, L0_conv_v3, L1_conv_norm1_w, L1_conv_norm1_b, L1_conv_qkv_w, L1_conv_proj_w, L1_conv_proj_b, L1_conv_cpb_w1, L1_conv_cpb_b1, L1_conv_cpb_w2, L1_conv_h_times, L1_conv_pow_para, L1_conv_ws_scalar, L1_conv_ws_scalar2, L1_conv_norm2_w, L1_conv_norm2_b, L1_conv_fc1_w, L1_conv_fc1_b, L1_conv_fc2_w, L1_conv_fc2_b):
    import jax
    import jax.numpy as jnp

    def _L0_conv_ref(x, w1, g1, b1, m1, v1, w2, g2, b2, m2, v2, w3, g3, b3, m3, v3):
        import jax, jax.numpy as jnp
        import numpy as np
        from jax import lax
        EPS = 0.001
        CARDINALITY = 32
        DN = ('NHWC', 'HWIO', 'NHWC')

        def _bn(x, gamma, beta, mean, var):
            return (x - mean) * lax.rsqrt(var + EPS) * gamma + beta
        h = lax.conv_general_dilated(x, w1, (1, 1), 'SAME', dimension_numbers=DN)
        h = jax.nn.relu(_bn(h, g1, b1, m1, v1))
        h = lax.conv_general_dilated(h, w2, (1, 1), 'SAME', feature_group_count=CARDINALITY, dimension_numbers=DN)
        h = jax.nn.relu(_bn(h, g2, b2, m2, v2))
        h = lax.conv_general_dilated(h, w3, (1, 1), 'SAME', dimension_numbers=DN)
        h = _bn(h, g3, b3, m3, v3)
        return jax.nn.relu(h + x)

    def _L1_conv_ref(x, norm1_w, norm1_b, qkv_w, proj_w, proj_b, cpb_w1, cpb_b1, cpb_w2, h_times, pow_para, ws_scalar, ws_scalar2, norm2_w, norm2_b, fc1_w, fc1_b, fc2_w, fc2_b):
        import jax, jax.numpy as jnp
        import numpy as np
        WS = (7, 7)
        SS = (3, 3)
        NUM_HEADS = 8
        NEG = -1000000000.0

        def _rel_index(ws):
            Wh, Ww = ws
            ch, cw = np.meshgrid(np.arange(Wh), np.arange(Ww), indexing='ij')
            coords = np.stack([ch, cw]).reshape(2, -1)
            rel = coords[:, :, None] - coords[:, None, :]
            rel = rel.transpose(1, 2, 0).astype(np.int64)
            rel[..., 0] += Wh - 1
            rel[..., 1] += Ww - 1
            rel[..., 0] *= 2 * Ww - 1
            return rel.sum(-1)

        def _swin_mask(H, W, ws, ss):
            img = np.zeros((H, W))
            hs = (slice(0, -ws[0]), slice(-ws[0], -ss[0]), slice(-ss[0], None)) if 0 < ss[0] < ws[0] else (slice(None),)
            wsl = (slice(0, -ws[1]), slice(-ws[1], -ss[1]), slice(-ss[1], None)) if 0 < ss[1] < ws[1] else (slice(None),)
            cnt = 0
            for h in hs:
                for w in wsl:
                    img[h, w] = cnt
                    cnt += 1
            m = img.reshape(H // ws[0], ws[0], W // ws[1], ws[1]).transpose(0, 2, 1, 3).reshape(-1, ws[0] * ws[1])
            diff = m[:, None, :] - m[:, :, None]
            return np.where(diff != 0, NEG, 0.0).astype(np.float32)

        def _coords_table(ws, h_times, ws_scalar, ws_scalar2, pow_para):
            Wh, Ww = ws
            ch = jnp.arange(-(Wh - 1), Wh, dtype=jnp.float32) / max(Wh - 1, 1)
            cw = jnp.arange(-(Ww - 1), Ww, dtype=jnp.float32) / max(Ww - 1, 1)
            tab = jnp.stack(jnp.meshgrid(ch, cw, indexing='ij'), axis=-1)
            tab = tab * h_times
            tab = jnp.sign(tab) * jnp.power(jnp.abs(tab) * ws_scalar + 1e-06, pow_para) / ws_scalar2
            return tab.reshape(-1, 2)

        def _ln(x, w, b):
            mu = x.mean(-1, keepdims=True)
            var = x.var(-1, keepdims=True)
            return (x - mu) / jnp.sqrt(var + 1e-05) * w + b
        B, H, W, C = x.shape
        h = NUM_HEADS
        d = C // h
        scale = d ** (-0.5)
        nWh, nWw = (H // WS[0], W // WS[1])
        nW = nWh * nWw
        N = WS[0] * WS[1]
        shortcut = x
        y = _ln(x, norm1_w, norm1_b)
        y = jnp.roll(y, (-SS[0], -SS[1]), axis=(1, 2))
        win = y.reshape(B, nWh, WS[0], nWw, WS[1], C).transpose(0, 1, 3, 2, 4, 5).reshape(B * nW, N, C)
        qkv = (win @ qkv_w.T).reshape(B * nW, N, 3, h, d).transpose(2, 0, 3, 1, 4)
        q, k, v = (qkv[0], qkv[1], qkv[2])
        attn = jnp.einsum('bhnd,bhmd->bhnm', q, k) * scale
        tab = _coords_table(WS, jax.nn.softplus(h_times), jax.nn.softplus(ws_scalar), jax.nn.softplus(ws_scalar2), jax.nn.sigmoid(pow_para))
        tb = jax.nn.relu(tab @ cpb_w1.T + cpb_b1) @ cpb_w2.T
        idx = jnp.asarray(_rel_index(WS))
        bias = tb[idx.reshape(-1)].reshape(N, N, h).transpose(2, 0, 1)
        attn = attn + bias[None]
        mask = jnp.asarray(_swin_mask(H, W, WS, SS))
        attn = attn.reshape(B, nW, h, N, N) + mask[None, :, None]
        attn = jax.nn.softmax(attn.reshape(B * nW, h, N, N), axis=-1)
        out = jnp.einsum('bhnm,bhmd->bhnd', attn, v).transpose(0, 2, 1, 3).reshape(B * nW, N, C)
        out = out @ proj_w.T + proj_b
        out = out.reshape(B, nWh, nWw, WS[0], WS[1], C).transpose(0, 1, 3, 2, 4, 5).reshape(B, H, W, C)
        out = jnp.roll(out, (SS[0], SS[1]), axis=(1, 2))
        x = shortcut + out
        z = _ln(x, norm2_w, norm2_b)
        z = jax.nn.gelu(z @ fc1_w.T + fc1_b, approximate=False) @ fc2_w.T + fc2_b
        return x + z

    def _gn(v, G=32, eps=1e-05):
        B_, H_, W_, C_ = v.shape
        g = v.reshape(B_, H_, W_, G, C_ // G)
        m = jnp.mean(g, axis=(1, 2, 4), keepdims=True)
        s = jnp.var(g, axis=(1, 2, 4), keepdims=True)
        return ((g - m) / jnp.sqrt(s + eps)).reshape(v.shape)

    def _ln_c(v, eps=1e-06):
        m = jnp.mean(v, axis=-1, keepdims=True)
        s = jnp.var(v, axis=-1, keepdims=True)
        return (v - m) / jnp.sqrt(s + eps)

    def _ln_t(v, eps=1e-05):
        m = jnp.mean(v, axis=-1, keepdims=True)
        s = jnp.var(v, axis=-1, keepdims=True)
        return (v - m) / jnp.sqrt(s + eps)

    def _to_tokens(v):
        B_, H_, W_, C_ = v.shape
        return v.reshape(B_, H_ * W_, C_)

    def _from_tokens(t, like):
        return t.reshape(like.shape)
    x = _L0_conv_ref(x, L0_conv_w1, L0_conv_g1, L0_conv_b1, L0_conv_m1, L0_conv_v1, L0_conv_w2, L0_conv_g2, L0_conv_b2, L0_conv_m2, L0_conv_v2, L0_conv_w3, L0_conv_g3, L0_conv_b3, L0_conv_m3, L0_conv_v3)
    x = _L1_conv_ref(x, L1_conv_norm1_w, L1_conv_norm1_b, L1_conv_qkv_w, L1_conv_proj_w, L1_conv_proj_b, L1_conv_cpb_w1, L1_conv_cpb_b1, L1_conv_cpb_w2, L1_conv_h_times, L1_conv_pow_para, L1_conv_ws_scalar, L1_conv_ws_scalar2, L1_conv_norm2_w, L1_conv_norm2_b, L1_conv_fc1_w, L1_conv_fc1_b, L1_conv_fc2_w, L1_conv_fc2_b)
    return x

_drawn_inputs = setup_inputs


def setup_inputs(seed=0):
    import zlib

    import numpy as np

    out = dict(_drawn_inputs(seed))
    spreads = {'L1_conv_norm1_w': (1.0, 0.6),
     'L1_conv_norm1_b': (0.0, 0.8),
     'L1_conv_proj_b': (0.0, 0.1),
     'L1_conv_cpb_b1': (0.0, 2.0),
     'L1_conv_norm2_w': (1.0, 0.6),
     'L1_conv_norm2_b': (0.0, 2.0),
     'L1_conv_fc1_b': (0.0, 0.638),
     'L1_conv_fc2_b': (0.0, 0.1)}
    factors = {'L0_conv_w1': 2.81,
     'L0_conv_g1': 8.0,
     'L0_conv_b1': 8.0,
     'L0_conv_m1': 8.0,
     'L0_conv_v1': 8.0,
     'L0_conv_g2': 8.0,
     'L0_conv_v2': 8.0,
     'L0_conv_g3': 6.162,
     'L0_conv_v3': 3.496,
     'L1_conv_qkv_w': 3.404,
     'L1_conv_proj_w': 3.391,
     'L1_conv_cpb_w1': 35.611,
     'L1_conv_cpb_w2': 48.101}
    for name, (base, spread) in spreads.items():
        noise = np.random.default_rng([zlib.crc32(name.encode()), seed]).standard_normal(out[name].shape)
        drawn = base * np.exp(spread * noise) if base else spread * noise
        out[name] = jnp.asarray(drawn.astype(out[name].dtype))
    for name, factor in factors.items():
        out[name] = (out[name] * factor).astype(out[name].dtype)
    return out
```

```python
import numpy as np
from collections import namedtuple
from contextlib import ExitStack

import concourse.bass as bass
from concourse import mybir

B, H, W, C = 32, 56, 56, 128
MID = 64
TAPS = 9
HEADS, D = 8, 16
WIN, SHIFT = 7, 3
N = WIN * WIN
STRIPS = H // WIN
WINS = W // WIN
PAIRS = WINS // 2
PT = 2 * N
ST = WINS * N
NS = B * STRIPS
QUADS = 4
HID = 4 * C
HC = HID // 128
REL = (2 * WIN - 1) ** 2
CPB = 256
BN_EPS, LN_EPS = 1e-3, 1e-5
NEG = -1e9

ROWS = 8
CHUNKS = H // ROWS
CT = 2 * W
TILES = ROWS * W // CT
CHT = ROWS * W
HP = W + 2
BPAIRS = B // 2

LEAD = 4
MOVES = PAIRS + 1


def shape_constants():
    c = {}
    c["ident"] = np.eye(128, dtype=np.float32)
    g = np.arange(-(WIN - 1), WIN, dtype=np.float32) / np.float32(WIN - 1)
    grid = np.stack([np.tile(g, 2 * WIN - 1), np.repeat(g, 2 * WIN - 1)], 0)
    c["coords"] = np.ascontiguousarray(grid[:, ::-1])
    img = np.zeros((H, W))
    cuts = (slice(0, -WIN), slice(-WIN, -SHIFT), slice(-SHIFT, None))
    for a, hs in enumerate(cuts):
        for b, ws in enumerate(cuts):
            img[hs, ws] = 3 * a + b
    m = img.reshape(STRIPS, WIN, WINS, WIN).transpose(0, 2, 3, 1).reshape(STRIPS, WINS, N)
    mask = np.where(m[:, :, None, :] != m[:, :, :, None], NEG, 0.0).astype(np.float32)
    both = mask[[0, STRIPS - 1]].transpose(2, 0, 1, 3)
    c["winmask"] = np.ascontiguousarray(np.concatenate([both, both], 0)).reshape(PT, 2 * WINS * N)
    ch = np.arange(C)
    c["headmask"] = np.stack([(ch // D % 2 == hh) * np.float32(D ** -0.5) for hh in range(2)], 1).astype(np.float32)
    row = np.arange(PT) // N
    c["vmask"] = np.broadcast_to((row[:, None, None] == (np.arange(HEADS) // 2 % 2)[None, :, None]),
                                 (PT, HEADS, D)).astype(np.float32).reshape(PT, HEADS * D)
    i, o = np.arange(2 * MID)[:, None], np.arange(2 * MID)[None, :]
    c["groupmask"] = (i // 2 == o // 2).astype(np.float32)
    return c






class Strip:

    def __init__(self, k, c):
        self.k, self.c = k, c
        self.fixed = isinstance(k, int)
        self.n = c if self.fixed else 2 * k + c
        self.u = c % 2
        self.half = c // 2 if self.fixed else k + c // 2

    def back(self, d):
        return Strip(self.k, self.c - d)

    def there(self):
        return not self.fixed or 0 <= self.c < NS


def wait(e, sem, value):
    if not isinstance(value, int) or value > 0:
        e.wait_ge(sem, value)


def over_strips(e, body):
    for c in range(-1, 5):
        body(Strip(0, c))
    with e.Fori(0, (NS - 6) // 2) as k:
        body(Strip(k, 5))
        body(Strip(k, 6))
    for c in range(NS - 1, NS + 3):
        body(Strip(0, c))


def over_chunks(e, step):
    for c in range(CHUNKS + 2):
        step(0, c)
    with e.Fori(1, BPAIRS) as gp:
        for c in range(CHUNKS + 2):
            step(gp, c)


PREP = ["abs", "exp", "ln", "positive", "softplus", "denominator", "sigmoid", "recip", "product", "magnitude",
        "sign", "scaled", "exponent", "power", "signed", "tab", "hidden_ps", "hidden", "table_ps", "table",
        "half", "quarter", "bn_var", "bn_rstd", "bn_scale", "bn_shift", "bn_bias",
        "b3_var", "b3_rstd", "b3_scale", "b3_shift", "b3_bias", "w3", "w2", "border", "ones", "pads"]


def program(nc, a, out):
    fp32 = mybir.dt.float32
    ALU = mybir.AluOpType
    ACT = mybir.ActivationFunctionType
    AX = mybir.AxisListType
    ctx = ExitStack()
    with ctx:
        def sb(name, shape):
            return ctx.enter_context(nc.sbuf_tensor(name, shape, fp32))

        def sem(name):
            return ctx.enter_context(nc.semaphore(name))

        x1_dram = nc.dram_tensor("x1_scratch", (B, H + SHIFT, W, C), fp32, kind="Internal").ap()
        tb_dram = nc.dram_tensor("tb_scratch", (HEADS, REL), fp32, kind="Internal").ap()

        ident = sb("ident_sb", [128, 128])
        headmask = sb("headmask_sb", [C, 2])
        vmask = sb("vmask_sb", [PT, HEADS, D])
        winmask = sb("winmask_sb", [PT, 2, WINS, N])
        groupmask = sb("groupmask_sb", [128, 2, MID])
        w1 = sb("w1_sb", [C, MID])
        w2raw = sb("w2raw", [128, TAPS, MID])
        w2 = sb("w2_sb", [128, TAPS, 2, MID])
        w3 = sb("w3_sb", [128, C])
        bn = sb("bn", [128, 4, 2])
        bn_var, bn_rstd, bn_scale, bn_shift, bn_bias = [sb(f"bn_{i}", [128, 2]) for i in range(5)]
        b3 = sb("b3", [128, 4, C])
        b3_var, b3_rstd, b3_scale, b3_shift, b3_bias = [sb(f"b3_{i}", [128, C]) for i in range(5)]
        wqkv = sb("wqkv", [C, 3 * C])
        wproj = sb("wproj", [C, C])
        projb = sb("projb", [PT, C])
        ln = sb("ln", [C, 4])
        fc1 = sb("fc1", [C, HID])
        fc1b = sb("fc1b", [128, HC])
        fc2 = sb("fc2", [128, HC, C])
        fc2b = sb("fc2b", [PT, C])
        half = sb("half", [128, C])
        quarter = sb("quarter", [PT, PAIRS])
        cpbw1 = sb("cpbw1", [2, CPB])
        cpbb1 = sb("cpbb1", [128, CPB // 128])
        cpbw2 = sb("cpbw2", [128, CPB // 128, HEADS])
        par = sb("par", [2, 4])
        par_abs, par_exp, par_ln, par_pos, par_sp = [sb(f"par_{i}", [2, 4]) for i in range(5)]
        sig_den, sig, ws2_recip = [sb(f"par1_{i}", [2, 1]) for i in range(3)]
        coords = sb("coords_sb", [2, REL])
        t_prod, t_mag, t_sign, t_scaled, t_exp, t_pow, t_signed, tab = [sb(f"tab{i}", [2, REL]) for i in range(8)]
        hid = sb("hid", [128, CPB // 128, REL])
        tb = sb("tb", [HEADS, REL])
        relb = sb("relb", [PT, QUADS, N])
        biasm = sb("biasm", [PT, 2, QUADS, WINS, N])

        xc = sb("xc", [CT, CHUNKS, 2, TILES, C])
        xct = sb("xct", [C, 2, CHT])
        h1 = sb("h1", [128, HP, HP])
        h2 = sb("h2", [128, 2, CHT])

        x1 = sb("x1", [PT, 2, PAIRS, C])
        xn = sb("xn", [PT, PAIRS, C])
        res1 = sb("res1", [PT, 2, PAIRS, C])
        res2 = sb("res2", [PT, 2, PAIRS, C])
        st = [sb(f"stats{i}", [PT, PAIRS, 6]) for i in range(2)]
        lnp = [sb(f"lnp{i}", [PT, 10, PAIRS]) for i in range(2)]
        xt = sb("xt", [C, WINS, 2, N])
        qm = sb("qm", [C, WINS, 2, N])
        kt = sb("kt", [C, WINS, N])
        vb = sb("vb", [PT, 2, WINS, HEADS, D + 1])
        sc = sb("sc", [PT, 2, 2, WINS, 2, N])
        mx = sb("mx", [PT, 2, WINS, 2])
        pt = sb("pt", [PT, WINS, 2, 2, 64])
        rsum = sb("rsum", [128, PAIRS, HEADS])
        on = sb("on", [128, PAIRS, C])
        ot = sb("ot", [C, PAIRS, PT])
        x2 = sb("x2", [PT, PAIRS, C])
        z = sb("z", [PT, PAIRS, C])
        zt = sb("zt", [C, ST])
        g = sb("g", [128, HC, ST])
        y = sb("y", [PT, 2, PAIRS, C])

        bank = [ctx.enter_context(nc.psum_tensor(f"bank{i}", [128, 512], fp32)) for i in range(8)]
        RA, RB, RC = bank[4], bank[5:7], bank[7]
        A_JOBS = 3
        B_JOBS = 5
        SMALL = 6
        C_JOBS = 6

        wload, prep, tb_store, tb_load = sem("wload"), sem("prep"), sem("tb_store"), sem("tb_load")
        xc_in = [sem(f"xc_in{c}") for c in range(CHUNKS)]
        xc_out = [sem(f"xc_out{c}") for c in range(CHUNKS)]
        xct_ps = [sem(f"xct_ps{m}") for m in range(2)]
        xct_sb = [sem(f"xct_sb{m}") for m in range(2)]
        conv3_ps = [sem(f"conv3_ps{m}") for m in range(2)]
        xc_biased, xc_summed, xc_relu = sem("xc_biased"), sem("xc_summed"), sem("xc_relu")
        conv1_ps, h1_sb, conv2_ps, h2_sb = sem("conv1_ps"), sem("h1_sb"), sem("conv2_ps"), sem("h2_sb")
        biasm_done = sem("biasm_done")
        x1_in = [sem(f"x1_in{u}") for u in range(2)]
        y_out = [sem(f"y_out{u}") for u in range(2)]
        stats = [sem(f"stats_sem{i}") for i in range(2)]
        small = [sem(f"small{i}") for i in range(2)]
        xn_sb, z_sb, res1_sb, res2_sb = sem("xn_sb"), sem("z_sb"), sem("res1_sb"), sem("res2_sb")
        a_full, a_out, c_full, c_out = sem("a_full"), sem("a_out"), sem("c_full"), sem("c_out")
        b_full = [sem(f"b_full{j}") for j in range(2)]
        b_out = [sem(f"b_out{j}") for j in range(2)]
        s_full, s_out, max_done, sub_done, exp_done = [sem(n) for n in
                                                       ("s_full", "s_out", "max_done", "sub_done", "exp_done")]
        rsum_done = sem("rsum_done")

        LOADS = []

        def b_before(t, job):
            if job == 0:
                return B_JOBS * t.n - (B_JOBS - 1)
            return B_JOBS * t.n + job + (1 if t.back(-1).there() else 0)

        def y_stored(u, n):
            return 16 * MOVES * n + (16 * MOVES * (WIN - 1) * (n // (STRIPS // 2)) if u else 0)

        block_ = ctx.enter_context(nc.Block())

        def at(e, name):
            wait(e, prep, PREP.index(name))

        @block_.sync
        def _(sp):
            def load(dst, src):
                LOADS.append(dst)
                sp.dma_start(dst, src).then_inc(wload, 16)

            def everywhere(name, parts, n=C):
                return bass.AP(tensor=a[name].tensor, offset=0, ap=[[0, parts], [1, n]])

            def column(name):
                return a[name].rearrange("(p o) -> p o", o=1)

            load(ident[:], a["ident"])
            load(w1[:], a["w1"])
            load(groupmask[:], a["groupmask"].rearrange("p (m o) -> p m o", m=2))
            for t in range(TAPS):
                load(w2raw[:, t, :], bass.AP(tensor=a["w2"].tensor, offset=t * 2 * MID,
                                             ap=[[0, MID], [MID, 2], [1, MID]]))
            for k in range(2):
                load(w3[MID * k:MID * k + MID, :], a["w3"])
                for l in range(2):
                    for i, nm in enumerate("gbmv"):
                        load(bn[MID * k:MID * k + MID, i, l:l + 1], column(f"{nm}{l + 1}"))
            for i, nm in enumerate("gbmv"):
                load(b3[:, i, :], everywhere(f"{nm}3", 128))
            load(headmask[:], a["headmask"])
            load(vmask[:], a["vmask"].rearrange("p (h d) -> p h d", h=HEADS))
            load(winmask[:].rearrange("p a w m -> p (a w m)"), a["winmask"])
            load(wqkv[:], a["qkv_wT"])
            load(wproj[:], a["proj_wT"])
            load(fc1[:], a["fc1_wT"])
            load(fc2[:], a["fc2_wT"].rearrange("(c p) n -> p c n", p=128))
            with nc.allow_non_contiguous_dma(reason="a few hundred elements, once"):
                load(fc1b[:], a["fc1_b"].rearrange("(c p) -> p c", p=128))
                load(cpbb1[:], a["cpb_b1"].rearrange("(c p) -> p c", p=128))
            load(projb[:], everywhere("proj_b", PT))
            load(fc2b[:], everywhere("fc2_b", PT))
            for i, nm in enumerate(("norm1_w", "norm1_b", "norm2_w", "norm2_b")):
                load(ln[:, i:i + 1], column(nm))
            load(coords[:], a["coords"])
            load(cpbw1[:], a["cpb_w1T"])
            load(cpbw2[:], a["cpb_w2T"].rearrange("(c p) n -> p c n", p=128))
            for i, nm in enumerate(("h_times", "ws_scalar", "ws_scalar2", "pow_para")):
                load(par[:, i:i + 1], everywhere(nm, 2, 1))

            def chunk(dram, gp, c, m):
                return dram[2 * gp + m, ROWS * c:ROWS * c + ROWS].rearrange("(t r) w ch -> (r w) t ch", t=TILES)

            def chunk_in(gp, c):
                for m in range(2):
                    sp.dma_start(xc[:, c, m], chunk(a["x"], gp, c, m)).then_inc(xc_in[c], 16)

            def chunk_out(gp, c):
                sp.wait_ge(xc_relu, 2 * (CHUNKS * gp + c + 1))
                for m in range(2):
                    sp.dma_start(chunk(x1_dram, gp, c, m), xc[:, c, m]).then_inc(xc_out[c], 16)
                    if c == 0:
                        sp.dma_start(x1_dram[2 * gp + m, H:H + 2].rearrange("r w c -> (r w) c"),
                                     xc[:, 0, m, 0, :]).then_inc(xc_out[0], 16)
                        sp.dma_start(x1_dram[2 * gp + m, H + 2], xc[0:W, 0, m, 1, :]).then_inc(xc_out[0], 16)

            for c in range(CHUNKS):
                chunk_in(0, c)
            sp.wait_ge(prep, PREP.index("table") + 1)
            sp.dma_start(tb_dram, tb[:]).then_inc(tb_store, 16)
            sp.wait_ge(tb_store, 16)
            for hh in range(2):
                for nj in range(WIN):
                    for ni in range(WIN):
                        first = REL - 1 - ((nj + WIN - 1) * (2 * WIN - 1) + ni + WIN - 1)
                        src = bass.AP(tensor=tb_dram.tensor, offset=hh * REL + first,
                                      ap=[[2 * REL, QUADS], [2 * WIN - 1, WIN], [1, WIN]])
                        n = hh * N + nj * WIN + ni
                        sp.dma_start(relb[n:n + 1], src) \
                            .then_inc(tb_load, 16)
            with sp.Fori(0, BPAIRS - 1) as gp:
                for c in range(CHUNKS + 2):
                    if c < CHUNKS:
                        chunk_out(gp, c)
                    if c >= 2:
                        sp.wait_ge(xc_out[c - 2], (32 if c > 2 else 96) * (gp + 1))
                        chunk_in(gp + 1, c - 2)
            for c in range(CHUNKS):
                chunk_out(BPAIRS - 1, c)
            for c in range(CHUNKS):
                sp.wait_ge(xc_out[c], (32 if c else 96) * BPAIRS)

            def columns(p):
                c0 = 2 * WIN * p + SHIFT
                if p < PAIRS - 1:
                    return [(c0, 0, 2 * WIN)]
                return [(c0, 0, W - c0), (0, W - c0, 2 * WIN - (W - c0))]

            def block(dram, img, r, c, nj):
                d = dram[img, bass.ds(r, WIN), c:c + nj, :]
                return d.rearrange("i j c -> j i c")

            def load_strip(img, s, u):
                n = STRIPS * img + s
                wait(sp, xn_sb, n - 1)
                wait(sp, res1_sb, n - 1)
                for p in range(PAIRS):
                    for c, j0, nj in columns(p):
                        sp.dma_start(x1[WIN * j0:WIN * (j0 + nj), u, p, :],
                                     block(x1_dram, img, WIN * s + SHIFT, c, nj)).then_inc(x1_in[u], 16)

            def store_strip(img, s, u, last=False):
                sp.wait_ge(c_out, C_JOBS * (STRIPS * img + s + 1))
                for p in range(PAIRS):
                    for c, j0, nj in columns(p):
                        if not last:
                            sp.dma_start(block(out, img, WIN * s + SHIFT, c, nj),
                                         y[WIN * j0:WIN * (j0 + nj), u, p, :]).then_inc(y_out[u], 16)
                            continue
                        for i in range(WIN):
                            rows = y[WIN * j0 + i:WIN * (j0 + nj - 1) + i + 1:WIN, u, p, :]
                            sp.dma_start(out[img, (WIN * s + SHIFT + i) % H, c:c + nj, :], rows).then_inc(y_out[u], 16)

            for s in range(LEAD):
                load_strip(0, s, s % 2)
            with sp.Fori(0, B - 1) as img:
                for s in range(STRIPS):
                    if s + LEAD < STRIPS:
                        load_strip(img, s + LEAD, s % 2)
                    else:
                        load_strip(img + 1, s + LEAD - STRIPS, s % 2)
                    store_strip(img, s, s % 2, s == STRIPS - 1)
            for s in range(STRIPS):
                if s + LEAD < STRIPS:
                    load_strip(B - 1, s + LEAD, s % 2)
                store_strip(B - 1, s, s % 2, s == STRIPS - 1)
            for u in range(2):
                sp.wait_ge(y_out[u], y_stored(u, NS // 2))

        @block_.tensor
        def _(pe):
            at(pe, "hidden_ps")
            for c in range(CPB // 128):
                mm = nc.tensor.matmul(bank[c][:, 0:REL], cpbw1[:, 128 * c:128 * c + 128], tab[:],
                                      start=True, stop=True)
            mm.then_inc(prep, 1)
            at(pe, "table_ps")
            for c in range(CPB // 128):
                mm = nc.tensor.matmul(bank[2][0:HEADS, 0:REL], cpbw2[:, c, :], hid[:, c, :],
                                      start=c == 0, stop=c == CPB // 128 - 1)
            mm.then_inc(prep, 1)

            pe.wait_ge(prep, len(PREP))

            def x_to_channels(gp, c):
                n = CHUNKS * gp + c
                pe.wait_ge(xc_in[c], 32 * (gp + 1))
                for m in range(2):
                    wait(pe, xct_sb[m], n)
                    for t in range(TILES):
                        mm = nc.tensor.transpose(bank[m][:, CT * t:CT * t + CT], xc[:, c, m, t, :],
                                                 ident[0:CT, 0:CT])
                    mm.then_inc(xct_ps[m], 1)

            def conv1(gp, c):
                n = CHUNKS * gp + c
                wait(pe, h1_sb, n)
                for m in range(2):
                    pe.wait_ge(xct_sb[m], n + 1)
                    mm = nc.tensor.matmul(bank[2][MID * m:MID * m + MID, 0:CHT], w1[:], xct[:, m, :],
                                          start=True, stop=True)
                mm.then_inc(conv1_ps, 1)

            def conv2(gp, c):
                n = CHUNKS * gp + c
                pe.wait_ge(h1_sb, n + (2 if c < CHUNKS - 1 else 1))
                wait(pe, h2_sb, n)
                for t in range(TAPS):
                    dy, dx = divmod(t, 3)
                    mm = nc.tensor.matmul(bank[3][:, 0:CHT], w2[:, t].rearrange("p m o -> p (m o)"),
                                          h1[:, ROWS * c + dy:ROWS * c + dy + ROWS, dx:dx + W],
                                          start=t == 0, stop=t == TAPS - 1)
                mm.then_inc(conv2_ps, 1)

            def conv3(gp, c):
                n = CHUNKS * gp + c
                pe.wait_ge(h2_sb, n + 1)
                wait(pe, xc_summed, 2 * n)
                for m in range(2):
                    for t in range(TILES):
                        mm = nc.tensor.matmul(bank[4 + m][0:CT, C * t:C * t + C],
                                              h2[MID * m:MID * m + MID, c % 2, CT * t:CT * t + CT],
                                              w3[MID * m:MID * m + MID, :], start=True, stop=True)
                    mm.then_inc(conv3_ps[m], 1)

            def convs(gp, c):
                if c == 0:
                    x_to_channels(gp, 0)
                if c < CHUNKS:
                    conv1(gp, c)
                if c + 1 < CHUNKS:
                    x_to_channels(gp, c + 1)
                if c >= 2:
                    conv3(gp, c - 2)
                if 1 <= c <= CHUNKS:
                    conv2(gp, c - 1)

            over_chunks(pe, convs)
            pe.wait_ge(h2_sb, CHUNKS * BPAIRS)
            pe.wait_ge(xc_summed, 2 * CHUNKS * BPAIRS)

            def to_channels(ring, src, full):
                for p in range(PAIRS):
                    mm = nc.tensor.transpose(ring[:, PT * p:PT * p + PT], src[:, p, :], ident[0:PT, 0:PT])
                mm.then_inc(full, 1)

            def values(t, j):
                wait(pe, b_out[j], b_before(t, 0))
                for w in range(4):
                    rows = xt[:, 4 * j + w].rearrange("c v n -> c (v n)")
                    mm = nc.tensor.matmul(RB[j][0:PT, C * w:C * w + C], rows, wqkv[:, 2 * C:3 * C],
                                          start=True, stop=True)
                mm.then_inc(b_full[j], 1)

            def project(t, i):
                wait(pe, a_out, A_JOBS * t.n + 1 + i)
                nc.tensor.matmul(RA[:, 0:ST], wqkv[:, C * i:C * i + C], xt[:, :, 0, :],
                                 start=True, stop=True).then_inc(a_full, 1)

            def scores(t):
                pe.wait_ge(a_out, A_JOBS * t.n + 3)
                wait(pe, s_out, QUADS * t.n)
                for w in range(WINS):
                    for q in range(QUADS):
                        mm = nc.tensor.matmul(bank[q][0:PT, N * w:N * w + N],
                                              qm[32 * q:32 * q + 32, w].rearrange("p h n -> p (h n)"),
                                              kt[32 * q:32 * q + 32, w, :], start=True, stop=True)
                mm.then_inc(s_full, 1)

            def probs_t(t, j):
                if j == 0:
                    pe.wait_ge(exp_done, t.n + 1)
                wait(pe, b_out[j % 2], b_before(t, 1 + j // 2))
                for v in range(2):
                    for r in range(2):
                        c0 = PT * (2 * v + r)
                        mm = nc.tensor.transpose(RB[j % 2][0:PT, c0:c0 + PT],
                                                 sc[:, t.u, r, 2 * j + v].rearrange("p q m -> p (q m)"), ident[0:PT, 0:PT])
                mm.then_inc(b_full[j % 2], 1)

            def attend(t, j):
                for i in range(2):
                    wait(pe, b_out[i], b_before(t, 3 if i == j or j == 1 else 2))
                o = RB[j][:, 0:2 * HEADS * (D + 1)].rearrange("p (k r q h d) -> p k r q h d", k=2, r=2, q=2, h=2)
                for k in range(2):
                    for v in range(2):
                        w = 2 * (2 * j + k) + v
                        val = vb[:, t.u, w].rearrange("p (r q h) d -> p r q h d", r=2, q=2)
                        for r in range(2):
                            for hh in range(2):
                                mm = nc.tensor.matmul(o[64 * v:64 * v + 64, k, r, :, hh, :], pt[:, w, r, hh, :],
                                                      val[:, r, :, hh, :], start=True, stop=True)
                mm.then_inc(b_full[j], 1)

            def attention_out(t):
                wait(pe, b_out[0], b_before(t, 4))
                wait(pe, b_out[1], b_before(t, 4))
                for p in range(PAIRS):
                    mm = nc.tensor.transpose(RB[0][:, 128 * p:128 * p + 128], on[:, p, :], ident[:])
                mm.then_inc(b_full[0], 1)

            def projection(t):
                wait(pe, b_out[0], b_before(t, 5))
                for p in range(PAIRS):
                    mm = nc.tensor.matmul(RB[1][0:PT, C * p:C * p + C], ot[:, p, :], wproj[:],
                                          start=True, stop=True)
                mm.then_inc(b_full[1], 1)

            def hidden(t, j):
                wait(pe, c_out, C_JOBS * t.n + 1 + j)
                nc.tensor.matmul(RC[:, 0:ST], fc1[:, 128 * j:128 * j + 128], zt[:],
                                 start=True, stop=True).then_inc(c_full, 1)

            def mlp_out(t):
                wait(pe, c_out, C_JOBS * t.n + 5)
                for p in range(PAIRS):
                    for c in range(HC):
                        mm = nc.tensor.matmul(RC[0:PT, C * p:C * p + C], g[:, c, PT * p:PT * p + PT],
                                              fc2[:, c, :], start=c == 0, stop=c == HC - 1)
                mm.then_inc(c_full, 1)

            def strips(t):
                ahead, t1, t2, t3 = t.back(-1), t.back(1), t.back(2), t.back(3)
                if t.there():
                    pe.wait_ge(a_out, A_JOBS * t.n + 1)
                    values(t, 0)
                    project(t, 0)
                if t3.there():
                    hidden(t3, 0)
                if t.there():
                    values(t, 1)
                    project(t, 1)
                if t3.there():
                    hidden(t3, 1)
                if t.there():
                    scores(t)
                if t1.there():
                    probs_t(t1, 0)
                if t3.there():
                    hidden(t3, 2)
                if t1.there():
                    probs_t(t1, 1)
                    probs_t(t1, 2)
                if t3.there():
                    hidden(t3, 3)
                if t1.there():
                    probs_t(t1, 3)
                    attend(t1, 0)
                    attend(t1, 1)
                if t3.there():
                    mlp_out(t3)
                if t1.there():
                    attention_out(t1)
                if ahead.there():
                    pe.wait_ge(xn_sb, ahead.n + 1)
                    wait(pe, a_out, A_JOBS * ahead.n)
                    to_channels(RA, xn, a_full)
                if t1.there():
                    projection(t1)
                if t2.there():
                    pe.wait_ge(z_sb, t2.n + 1)
                    wait(pe, c_out, C_JOBS * t2.n)
                    to_channels(RC, z, c_full)

            over_strips(pe, strips)

        @block_.scalar
        def _(act):
            def step(name, *args, **kw):
                at(act, name)
                nc.scalar.activation(*args, **kw).then_inc(prep, 1)

            act.wait_ge(wload, 16 * len(LOADS))
            step("abs", par_abs[:, 0:3], par[:, 0:3], ACT.Abs)
            at(act, "exp")
            nc.scalar.activation(par_exp[:, 3:4], par[:, 3:4], ACT.Exp, scale=-1.0)
            nc.scalar.activation(par_exp[:, 0:3], par_abs[:, 0:3], ACT.Exp, scale=-1.0).then_inc(prep, 1)
            step("ln", par_ln[:, 0:3], par_exp[:, 0:3], ACT.Ln, bias=1.0)
            step("magnitude", t_mag[:], t_prod[:], ACT.Abs)
            step("sign", t_sign[:], t_prod[:], ACT.Sign)
            at(act, "hidden")
            for c in range(CPB // 128):
                i = nc.scalar.activation(hid[:, c, :], bank[c][:, 0:REL], ACT.Relu, bias=cpbb1[:, c:c + 1])
            i.then_inc(prep, 1)
            step("table", tb[:], bank[2][0:HEADS, 0:REL], ACT.Copy)

            act.wait_ge(prep, len(PREP))

            def xct_out(gp, c):
                n = CHUNKS * gp + c
                act.wait_ge(xct_ps[0], n + 1)
                wait(act, conv1_ps, n)
                nc.scalar.activation(xct[:, 0, :], bank[0][:, 0:CHT], ACT.Copy).then_inc(xct_sb[0], 1)

            def h1_out(gp, c):
                act.wait_ge(conv1_ps, CHUNKS * gp + c + 1)
                nc.scalar.activation(h1[:, 1 + ROWS * c:1 + ROWS * c + ROWS, 1:1 + W],
                                     bank[2][:, 0:CHT].rearrange("p (r w) -> p r w", w=W), ACT.Relu,
                                     scale=bn_scale[:, 0:1], bias=bn_bias[:, 0:1]).then_inc(h1_sb, 1)

            def h2_out(gp, c):
                n = CHUNKS * gp + c
                act.wait_ge(conv2_ps, n + 1)
                wait(act, conv3_ps[1], n if c == 0 else CHUNKS * gp + max(c - 1, 0))
                nc.scalar.activation(h2[:, c % 2, :], bank[3][:, 0:CHT], ACT.Relu,
                                     scale=bn_scale[:, 1:2], bias=bn_bias[:, 1:2]).then_inc(h2_sb, 1)

            def relu_out(gp, c):
                n = CHUNKS * gp + c
                for m in range(2):
                    act.wait_ge(xc_summed, 2 * n + m + 1)
                    nc.scalar.activation(xc[:, c, m], xc[:, c, m], ACT.Relu).then_inc(xc_relu, 1)

            def convs(gp, c):
                if c == 0:
                    xct_out(gp, 0)
                if c < CHUNKS:
                    h1_out(gp, c)
                if c + 1 < CHUNKS:
                    xct_out(gp, c + 1)
                if c >= 2:
                    relu_out(gp, c - 2)
                if 1 <= c <= CHUNKS:
                    h2_out(gp, c - 1)

            over_chunks(act, convs)

            def xt_out(t):
                act.wait_ge(a_full, A_JOBS * t.n + 1)
                for v in range(2):
                    i = nc.scalar.activation(xt[:, :, v, :], RA[:, 0:ST].rearrange("c (w n) -> c w n", n=N),
                                             ACT.Identity, scale=ln[:, 0:1], bias=ln[:, 1:2])
                i.then_inc(a_out, 1)

            def q_out(t):
                act.wait_ge(a_full, A_JOBS * t.n + 2)
                wait(act, s_full, t.n)
                for hh in range(2):
                    i = nc.scalar.activation(qm[:, :, hh, :], RA[:, 0:ST].rearrange("c (w n) -> c w n", n=N),
                                             ACT.Identity, scale=headmask[:, hh:hh + 1])
                i.then_inc(a_out, 1)

            def k_out(t):
                act.wait_ge(a_full, A_JOBS * t.n + 3)
                nc.scalar.activation(kt[:].rearrange("c w n -> c (w n)"), RA[:, 0:ST], ACT.Copy).then_inc(a_out, 1)

            def zt_out(t):
                act.wait_ge(c_full, C_JOBS * t.n + 1)
                nc.scalar.activation(zt[:], RC[:, 0:ST], ACT.Identity, scale=ln[:, 2:3],
                                     bias=ln[:, 3:4]).then_inc(c_out, 1)

            def gelu(t, j):
                act.wait_ge(c_full, C_JOBS * t.n + 2 + j)
                nc.scalar.activation(g[:, j, :], RC[:, 0:ST], ACT.Gelu, bias=fc1b[:, j:j + 1]).then_inc(c_out, 1)

            def pt_out(t, j):
                act.wait_ge(b_full[j % 2], b_before(t, 1 + j // 2) + 1)
                nc.scalar.activation(pt[:, 2 * j:2 * j + 2, :, :, 0:N].rearrange("p v r h n -> p (v r h) n"),
                                     RB[j % 2][0:PT, 0:4 * PT].rearrange("p (b n) -> p b n", n=N),
                                     ACT.Copy).then_inc(b_out[j % 2], 1)

            def ot_out(t):
                act.wait_ge(b_full[0], b_before(t, 4) + 1)
                wait(act, b_full[1], b_before(t, 4))
                nc.scalar.activation(ot[:].rearrange("c p (v n) -> c (p v) n", v=2),
                                     RB[0][:].rearrange("c (w n) -> c w n", n=64)[:, :, 0:N],
                                     ACT.Copy).then_inc(b_out[0], 1)

            def exponentials(t):
                for r in range(2):
                    act.wait_ge(sub_done, 2 * t.n + r + 1)
                    half_sc = sc[:, t.u, r].rearrange("p w q m -> p (w q m)")
                    i = nc.scalar.activation(half_sc, half_sc, ACT.Exp)
                i.then_inc(exp_done, 1)

            def strips(t):
                ahead, t1, t2, t3 = t.back(-1), t.back(1), t.back(2), t.back(3)
                if t.there():
                    q_out(t)
                if t3.there():
                    gelu(t3, 0)
                if t.there():
                    k_out(t)
                if t3.there():
                    gelu(t3, 1)
                if t1.there():
                    pt_out(t1, 0)
                if t3.there():
                    gelu(t3, 2)
                if t1.there():
                    pt_out(t1, 1)
                    pt_out(t1, 2)
                if t3.there():
                    gelu(t3, 3)
                if t1.there():
                    pt_out(t1, 3)
                if t.there():
                    exponentials(t)
                if t1.there():
                    ot_out(t1)
                if ahead.there():
                    xt_out(ahead)
                if t2.there():
                    zt_out(t2)

            over_strips(act, strips)

        def norm_stats(i, t, src):
            for p in range(PAIRS):
                ins = nc.vector.bn_stats(st[i][:, p, :], src[:, p, :])
            ins.then_inc(stats[i], 1)

        @block_.vector
        def _(dve):
            def step(name, f, *args, **kw):
                at(dve, name)
                f(*args, **kw).then_inc(prep, 1)

            V = nc.vector
            step("positive", V.tensor_scalar, par_pos[:, 0:3], par[:, 0:3], 0.0, None, ALU.max)
            step("softplus", V.tensor_tensor, out=par_sp[:, 0:3], in0=par_pos[:, 0:3], in1=par_ln[:, 0:3], op=ALU.add)
            step("denominator", V.tensor_scalar, sig_den[:], par_exp[:, 3:4], 1.0, None, ALU.add)
            step("sigmoid", V.reciprocal, sig[:], sig_den[:])
            step("recip", V.reciprocal, ws2_recip[:], par_sp[:, 2:3])
            step("product", V.tensor_scalar, t_prod[:], coords[:], par_sp[:, 0:1], None, ALU.mult)
            step("scaled", V.tensor_scalar, t_scaled[:], t_mag[:], par_sp[:, 1:2], 1e-6, ALU.mult, ALU.add)
            step("exponent", V.tensor_copy, t_exp[:], sig[:].to_broadcast([2, REL]))
            step("signed", V.tensor_tensor, out=t_signed[:], in0=t_sign[:], in1=t_pow[:], op=ALU.mult)
            step("tab", V.tensor_scalar, tab[:], t_signed[:], ws2_recip[:], None, ALU.mult)
            at(dve, "w2")
            for t in range(TAPS):
                i = V.tensor_tensor(out=w2[:, t], in0=w2raw[:, t].unsqueeze(1).to_broadcast([128, 2, MID]),
                                    in1=groupmask[:], op=ALU.mult)
            i.then_inc(prep, 1)
            step("border", V.memset, h1[:], 0.0)
            at(dve, "ones")
            for u in range(2):
                i = V.tensor_copy(vb[:, u, :, :, D], vmask[:, :, 0].unsqueeze(1).to_broadcast([PT, WINS, HEADS]))
            i.then_inc(prep, 1)
            step("pads", V.memset, pt[:, :, :, :, N:64].rearrange("p w r h n -> p (w r h) n"), 1.0)

            dve.wait_ge(prep, len(PREP))

            def xct_out(gp, c):
                n = CHUNKS * gp + c
                dve.wait_ge(xct_ps[1], n + 1)
                wait(dve, conv1_ps, n)
                V.tensor_copy(xct[:, 1, :], bank[1][:, 0:CHT]).then_inc(xct_sb[1], 1)

            def sum_out(gp, c):
                n = CHUNKS * gp + c
                dve.wait_ge(xc_biased, n + 1)
                for m in range(2):
                    dve.wait_ge(conv3_ps[m], n + 1)
                    x_m = xc[:, c, m].rearrange("p t c -> p (t c)")
                    V.tensor_tensor(out=x_m, in0=bank[4 + m][0:CT, :], in1=x_m, op=ALU.add).then_inc(xc_summed, 1)

            def convs(gp, c):
                if c == 0:
                    xct_out(gp, 0)
                if c + 1 < CHUNKS:
                    xct_out(gp, c + 1)
                if c >= 2:
                    sum_out(gp, c - 2)

            over_chunks(dve, convs)

            dve.wait_ge(tb_load, 16 * PT)
            for kind in range(2):
                for q in range(QUADS):
                    i = V.tensor_tensor(out=biasm[:, kind, q], in0=winmask[:, kind],
                                        in1=relb[:, q].unsqueeze(1).to_broadcast([PT, WINS, N]), op=ALU.add)
            i.then_inc(biasm_done, 1)
            dve.wait_ge(biasm_done, 1)

            def v_out(t, j):
                dve.wait_ge(b_full[j], b_before(t, 0) + 1 if t.c or not t.fixed else 1)
                V.tensor_tensor(out=vb[:, t.u, 4 * j:4 * j + 4, :, 0:D],
                                in0=RB[j][0:PT, :].rearrange("p (w h d) -> p w h d", w=4, h=HEADS),
                                in1=vmask[:].unsqueeze(1).to_broadcast([PT, 4, HEADS, D]),
                                op=ALU.mult).then_inc(b_out[j], 1)

            def biased(t):
                dve.wait_ge(s_full, t.n + 1)
                for q in range(QUADS):
                    if t.u == 0:
                        b = biasm[:, 0, q]
                    elif t.fixed:
                        b = biasm[:, int(t.n % STRIPS == STRIPS - 1), q]
                    else:
                        b = biasm[:, bass.ds((t.half % (STRIPS // 2)) // (STRIPS // 2 - 1), 1), q]
                        b = b.rearrange("p o w m -> p (o w) m")
                    V.tensor_tensor(out=sc[:, t.u, q // 2, :, q % 2, :],
                                    in0=bank[q][0:PT, 0:ST].rearrange("p (w m) -> p w m", m=N),
                                    in1=b, op=ALU.add).then_inc(s_out, 1)

            def maxima(t):
                wait(dve, sub_done, 2 * t.n)
                for r in range(2):
                    dve.wait_ge(s_out, QUADS * t.n + 2 * r + 2)
                    V.reduce_max(mx[:, r].rearrange("p w q -> p (w q)"),
                                 sc[:, t.u, r].rearrange("p w q m -> p (w q) m"), AX.X).then_inc(max_done, 1)

            def normalise(t, j):
                dve.wait_ge(b_full[j], b_before(t, 3) + 1)
                wait(dve, b_full[0], b_before(t.back(1), 5) if not (t.fixed and t.c == 0) else 0)
                o = RB[j][:, 0:2 * HEADS * (D + 1)].rearrange("p (k h d) -> p k h d", k=2, h=HEADS)
                V.reciprocal(rsum[:, 2 * j:2 * j + 2, :], o[:, :, :, D]).then_inc(rsum_done, 1)
                dve.wait_ge(rsum_done, 2 * t.n + j + 1)
                V.tensor_tensor(out=on[:, 2 * j:2 * j + 2, :].rearrange("p k (h d) -> p k h d", h=HEADS),
                                in0=o[:, :, :, 0:D],
                                in1=rsum[:, 2 * j:2 * j + 2, :].unsqueeze(3).to_broadcast([128, 2, HEADS, D]),
                                op=ALU.mult).then_inc(b_out[j], 1)

            def x1_stats(t):
                dve.wait_ge(x1_in[t.u], 16 * MOVES * (t.half + 1))
                wait(dve, small[0], SMALL * t.n)
                norm_stats(0, t, x1[:, t.u])

            def norm(i, t, src, dst, done):
                dve.wait_ge(small[i], SMALL * t.n + SMALL)
                for p in range(PAIRS):
                    ins = V.tensor_scalar(dst[:, p, :], src[:, p, :], lnp[i][:, 8, p:p + 1], lnp[i][:, 9, p:p + 1],
                                          ALU.mult, ALU.add)
                ins.then_inc(done, 1)

            def x1_norm(t):
                wait(dve, a_full, A_JOBS * (t.n - 1) + 1)
                norm(0, t, x1[:, t.u], xn, xn_sb)

            def x2_norm(t):
                wait(dve, c_full, C_JOBS * (t.n - 1) + 1)
                norm(1, t, x2, z, z_sb)

            def x2_out(t):
                dve.wait_ge(b_full[1], b_before(t, 4) + 1)
                dve.wait_ge(res1_sb, t.n + 1)
                wait(dve, res2_sb, t.n)
                V.tensor_tensor(out=x2[:].rearrange("p k c -> p (k c)"), in0=RB[1][0:PT, :],
                                in1=res1[:, t.u].rearrange("p k c -> p (k c)"), op=ALU.add).then_inc(b_out[1], 1)
                dve.wait_ge(b_out[1], b_before(t, 5))
                norm_stats(1, t, x2)

            def y_sum(t):
                dve.wait_ge(c_full, C_JOBS * t.n + 6)
                wait(dve, y_out[t.u], y_stored(t.u, t.half))
                dve.wait_ge(res2_sb, t.n + 1)
                V.tensor_tensor(out=y[:, t.u].rearrange("p k c -> p (k c)"), in0=RC[0:PT, :],
                                in1=res2[:, t.u].rearrange("p k c -> p (k c)"), op=ALU.add).then_inc(c_out, 1)

            def strips(t):
                ahead, t1, t2, t3 = t.back(-1), t.back(1), t.back(2), t.back(3)
                if t.there():
                    v_out(t, 0)
                if ahead.there():
                    x1_stats(ahead)
                if t.there():
                    v_out(t, 1)
                if t2.there():
                    x2_norm(t2)
                if ahead.there():
                    x1_norm(ahead)
                if t.there():
                    biased(t)
                    maxima(t)
                if t1.there():
                    normalise(t1, 0)
                    normalise(t1, 1)
                if t3.there():
                    y_sum(t3)
                if t1.there():
                    x2_out(t1)

            over_strips(dve, strips)

        @block_.gpsimd
        def _(pool):
            P = nc.gpsimd

            def step(name, f, *args, **kw):
                at(pool, name)
                f(*args, **kw).then_inc(prep, 1)

            def tt(o, x, y_, op):
                return P.tensor_tensor(out=o, in0=x, in1=y_, op=op)

            step("power", tt, t_pow[:], t_scaled[:], t_exp[:], ALU.pow)
            step("half", P.memset, half[:], -0.5)
            step("quarter", P.memset, quarter[:], 0.25)
            for n, v, shift_, rstd_, scale_, bias_, q in (
                    ("bn", bn, bn_shift, bn_rstd, bn_scale, bn_bias, bn_var),
                    ("b3", b3, b3_shift, b3_rstd, b3_scale, b3_bias, b3_var)):
                step(f"{n}_var", P.tensor_scalar, q[:], v[:, 3], BN_EPS, None, ALU.add)
                step(f"{n}_rstd", tt, rstd_[:], q[:], half[:, 0:q.shape[1]], ALU.pow)
                step(f"{n}_scale", tt, scale_[:], v[:, 0], rstd_[:], ALU.mult)
                step(f"{n}_shift", tt, shift_[:], v[:, 2], scale_[:], ALU.mult)
                step(f"{n}_bias", tt, bias_[:], v[:, 1], shift_[:], ALU.subtract)
            step("w3", tt, w3[:], w3[:], b3_scale[:], ALU.mult)

            def convs(gp, c):
                if c < CHUNKS:
                    n = CHUNKS * gp + c
                    pool.wait_ge(xct_ps[1], n + 1)
                    x_c = xc[:, c].rearrange("p m t c -> p (m t) c")
                    P.tensor_tensor(out=x_c, in0=x_c, in1=b3_bias[0:CT].unsqueeze(1).to_broadcast(
                        [CT, 2 * TILES, C]), op=ALU.add).then_inc(xc_biased, 1)

            pool.wait_ge(prep, len(PREP))
            over_chunks(pool, convs)

            def factors(i, t, x):
                _, mean_e, dev_e, _, mean_o, dev_o = [st[i][:, :, k] for k in range(6)]
                sum_, dif, dev, dif2, dev_eps, dif4, var, negm, rstd, shift = [lnp[i][:, k] for k in range(10)]
                pool.wait_ge(stats[i], t.n + 1)
                tt(sum_, mean_e, mean_o, ALU.add)
                tt(dif, mean_e, mean_o, ALU.subtract)
                tt(dev, dev_e, dev_o, ALU.add).then_inc(small[i], 1)
                pool.wait_ge(small[i], SMALL * t.n + 1)
                tt(dif2, dif, dif, ALU.mult)
                P.tensor_scalar(dev_eps, dev, 1.0 / C, LN_EPS, ALU.mult, ALU.add)
                tt(negm, sum_, half[0:PT, 0:PAIRS], ALU.mult).then_inc(small[i], 1)
                pool.wait_ge(small[i], SMALL * t.n + 2)
                tt(dif4, dif2, quarter[:], ALU.mult).then_inc(small[i], 1)
                pool.wait_ge(small[i], SMALL * t.n + 3)
                tt(var, dif4, dev_eps, ALU.add).then_inc(small[i], 1)
                pool.wait_ge(small[i], SMALL * t.n + 4)
                wait(pool, x, t.n)
                tt(rstd, var, half[0:PT, 0:PAIRS], ALU.pow).then_inc(small[i], 1)
                pool.wait_ge(small[i], SMALL * t.n + 5)
                tt(shift, negm, rstd, ALU.mult).then_inc(small[i], 1)

            def add_bias(res, src, bias, done):
                P.tensor_tensor(out=res, in0=src, in1=bias[:].unsqueeze(1).to_broadcast([PT, PAIRS, C]),
                                op=ALU.add).then_inc(done, 1)

            def residual1(t):
                pool.wait_ge(stats[0], t.n + 1)
                wait(pool, b_out[1], b_before(t.back(2), 5) if t.back(2).there() else 0)
                add_bias(res1[:, t.u], x1[:, t.u], projb, res1_sb)

            def residual2(t):
                pool.wait_ge(b_out[1], b_before(t, 5))
                wait(pool, c_out, C_JOBS * (t.n - 1))
                add_bias(res2[:, t.u], x2[:], fc2b, res2_sb)

            def subtract(t):
                for r in range(2):
                    pool.wait_ge(max_done, 2 * t.n + r + 1)
                    s_r = sc[:, t.u, r].rearrange("p w q m -> p (w q) m")
                    m_r = mx[:, r].rearrange("p w q -> p (w q)").unsqueeze(2)
                    P.tensor_tensor(out=s_r, in0=s_r, in1=m_r.to_broadcast([PT, 2 * WINS, N]),
                                    op=ALU.subtract).then_inc(sub_done, 1)

            def strips(t):
                ahead, t2 = t.back(-1), t.back(2)
                if t2.there():
                    factors(1, t2, z_sb)
                if ahead.there():
                    factors(0, ahead, xn_sb)
                if t2.there():
                    residual2(t2)
                if t.there():
                    subtract(t)
                if ahead.there():
                    residual1(ahead)

            over_strips(pool, strips)


_OUT = (B, H, W, C)


def kernel(**inputs):
    import concourse.bacc as bacc
    from concourse.bass_utils import run_bass_kernel_spmd as run

    def arr(name):
        return np.ascontiguousarray(inputs[name])

    arrays = {"x": arr("x")}
    for i in "123":
        for v in "gbmv":
            arrays[v + i] = arr(f"L0_conv_{v}{i}")
    arrays["w1"] = arr("L0_conv_w1").reshape(C, MID)
    arrays["w2"] = arr("L0_conv_w2").reshape(-1)
    arrays["w3"] = arr("L0_conv_w3").reshape(MID, C)
    for v in ("norm1_w", "norm1_b", "norm2_w", "norm2_b", "proj_b", "fc1_b", "fc2_b", "cpb_b1"):
        arrays[v] = arr("L1_conv_" + v)
    for v in ("h_times", "pow_para", "ws_scalar", "ws_scalar2"):
        arrays[v] = arr("L1_conv_" + v).reshape(1)
    for v in ("qkv_w", "proj_w", "fc1_w", "fc2_w", "cpb_w1", "cpb_w2"):
        arrays[v + "T"] = np.ascontiguousarray(arr("L1_conv_" + v).T)
    arrays.update(shape_constants())

    nc = bacc.Bacc("TRN2", target_bir_lowering=False, num_devices=1)
    handles = {n: nc.dram_tensor("in_" + n, v.shape, mybir.dt.float32, kind="ExternalInput").ap()
               for n, v in arrays.items()}
    out = nc.dram_tensor("out_x", _OUT, mybir.dt.float32, kind="ExternalOutput").ap()
    program(nc, handles, out)
    r = run(nc, [{"in_" + n: v for n, v in arrays.items()}], core_ids=[0])
    return r.results[0]["out_x"]
```

```python
import numpy as np
from collections import namedtuple
from contextlib import ExitStack

import concourse.bass as bass
from concourse import mybir

B, H, W, C = 32, 56, 56, 128
MID = 64
TAPS = 9
HEADS, D = 8, 16
WIN, SHIFT = 7, 3
N = WIN * WIN
STRIPS = H // WIN
WINS = W // WIN
PAIRS = WINS // 2
PT = 2 * N
ST = WINS * N
NS = B * STRIPS
QUADS = 4
QROWS = 64
HID = 4 * C
HC = HID // 128
REL = (2 * WIN - 1) ** 2
CPB = 256
BN_EPS, LN_EPS = 1e-3, 1e-5
NEG = -1e9

ROWS = 8
CHUNKS = H // ROWS
CT = 2 * W
TILES = ROWS * W // CT
CHT = ROWS * W
HP = W + 2
BPAIRS = B // 2

LEAD = 5
MOVES = PAIRS + 1


def shape_constants():
    c = {}
    c["ident"] = np.eye(128, dtype=np.float32)
    g = np.arange(-(WIN - 1), WIN, dtype=np.float32) / np.float32(WIN - 1)
    grid = np.stack([np.tile(g, 2 * WIN - 1), np.repeat(g, 2 * WIN - 1)], 0)
    c["coords"] = np.ascontiguousarray(grid[:, ::-1])
    img = np.zeros((H, W))
    cuts = (slice(0, -WIN), slice(-WIN, -SHIFT), slice(-SHIFT, None))
    for a, hs in enumerate(cuts):
        for b, ws in enumerate(cuts):
            img[hs, ws] = 3 * a + b
    m = img.reshape(STRIPS, WIN, WINS, WIN).transpose(0, 2, 3, 1).reshape(STRIPS, WINS, N)
    mask = np.where(m[:, :, None, :] != m[:, :, :, None], NEG, 0.0).astype(np.float32)
    both = mask[[0, STRIPS - 1]].transpose(2, 0, 1, 3)
    winmask = np.zeros((2, QROWS, 2, PAIRS, N), np.float32)
    for v in range(2):
        winmask[v, :N] = both[:, :, v::2]
    c["winmask"] = winmask.reshape(2 * QROWS, 2 * PAIRS * N)
    ch = np.arange(C)
    c["headmask"] = np.stack([(ch // D % 2 == hh) * np.float32(D ** -0.5) for hh in range(2)], 1).astype(np.float32)
    row = np.arange(PT) // N
    c["vmask"] = np.broadcast_to((row[:, None, None] == (np.arange(HEADS) % 2)[None, :, None]),
                                 (PT, HEADS, D)).astype(np.float32).reshape(PT, HEADS * D)
    i, o = np.arange(2 * MID)[:, None], np.arange(2 * MID)[None, :]
    c["groupmask"] = (i // 2 == o // 2).astype(np.float32)
    return c






class Strip:

    def __init__(self, k, c):
        self.k, self.c = k, c
        self.fixed = isinstance(k, int)
        self.n = c if self.fixed else 2 * k + c
        self.u = c % 2
        self.half = c // 2 if self.fixed else k + c // 2

    def back(self, d):
        return Strip(self.k, self.c - d)

    def there(self):
        return not self.fixed or 0 <= self.c < NS


def wait(e, sem, value):
    if not isinstance(value, int) or value > 0:
        e.wait_ge(sem, value)


def over_strips(e, body):
    for c in range(-1, 5):
        body(Strip(0, c))
    with e.Fori(0, (NS - 6) // 2) as k:
        body(Strip(k, 5))
        body(Strip(k, 6))
    for c in range(NS - 1, NS + 3):
        body(Strip(0, c))


def over_chunks(e, step, bias_steps):
    for c in range(CHUNKS + 2):
        step(0, c)
        bias_steps(c)
    with e.Fori(1, BPAIRS) as gp:
        for c in range(CHUNKS + 2):
            step(gp, c)


CONV_PREP = ["border", "half", "quarter", "relb_clear", "qt_clear",
             "bn_var", "bn_rstd", "bn_scale", "bn_shift", "bn_bias",
             "b3_var", "b3_rstd", "b3_scale", "b3_shift", "b3_bias", "w3", "w2", "w2_hi", "w2_lo"]
BIAS_PREP = ["abs", "exp", "ln", "positive", "softplus", "denominator", "sigmoid", "recip", "product", "magnitude",
             "sign", "scaled", "exponent", "power", "signed", "tab", "hidden_ps", "hidden", "table_ps", "table", "ones"]
PREP = CONV_PREP + BIAS_PREP


def program(nc, a, out):
    fp32 = mybir.dt.float32
    fp32r = mybir.dt.float32r
    ALU = mybir.AluOpType
    ACT = mybir.ActivationFunctionType
    AX = mybir.AxisListType
    ctx = ExitStack()
    with ctx:
        def sb(name, shape, dtype=fp32):
            return ctx.enter_context(nc.sbuf_tensor(name, shape, dtype))

        def sem(name):
            return ctx.enter_context(nc.semaphore(name))

        x1_dram = nc.dram_tensor("x1_scratch", (B, H + SHIFT, W, C), fp32, kind="Internal").ap()
        tb_dram = nc.dram_tensor("tb_scratch", (HEADS, REL), fp32, kind="Internal").ap()

        ident = sb("ident_sb", [128, 128])
        headmask = sb("headmask_sb", [C, 2])
        vmask = sb("vmask_sb", [PT, HEADS, D])
        winmask = sb("winmask_sb", [128, 2, PAIRS, N])
        groupmask = sb("groupmask_sb", [128, 2, MID])
        w1 = sb("w1_sb", [C, MID])
        w2raw = sb("w2raw", [128, TAPS, MID])
        w2 = sb("w2_sb", [128, TAPS, 2, MID])
        w2_hi, w2_lo = [sb(f"w2_{i}", [128, TAPS, 2 * MID], fp32r) for i in ("hi", "lo")]
        w3 = sb("w3_sb", [128, C])
        bn = sb("bn", [128, 4, 2])
        bn_var, bn_rstd, bn_scale, bn_shift, bn_bias = [sb(f"bn_{i}", [128, 2]) for i in range(5)]
        b3 = sb("b3", [128, 4, C])
        b3_var, b3_rstd, b3_scale, b3_shift, b3_bias = [sb(f"b3_{i}", [128, C]) for i in range(5)]
        wqkv = sb("wqkv", [C, 3 * C])
        wproj = sb("wproj", [C, C])
        projb = sb("projb", [PT, C])
        ln = sb("ln", [C, 4])
        fc1 = sb("fc1", [C, HID])
        fc1b = sb("fc1b", [128, HC])
        fc2 = sb("fc2", [128, HC, C])
        fc2b = sb("fc2b", [PT, C])
        half = sb("half", [128, C])
        quarter = sb("quarter", [PT, PAIRS])
        cpbw1 = sb("cpbw1", [2, CPB])
        cpbb1 = sb("cpbb1", [128, CPB // 128])
        cpbw2 = sb("cpbw2", [128, CPB // 128, HEADS])
        par = sb("par", [2, 4])
        par_abs, par_exp, par_ln, par_pos, par_sp = [sb(f"par_{i}", [2, 4]) for i in range(5)]
        sig_den, sig, ws2_recip = [sb(f"par1_{i}", [2, 1]) for i in range(3)]
        coords = sb("coords_sb", [2, REL])
        t_prod, t_mag, t_sign, t_scaled, t_exp, t_pow, t_signed, tab = [sb(f"tab{i}", [2, REL]) for i in range(8)]
        hid = sb("hid", [128, CPB // 128, REL])
        tb = sb("tb", [HEADS, REL])
        relb = sb("relb", [128, HEADS, N])
        biasm = sb("biasm", [128, 2, QUADS, PAIRS, 2, N])

        xc = sb("xc", [CT, CHUNKS, 2, TILES, C])
        xct = sb("xct", [C, 2, CHT])
        h1 = sb("h1", [128, 2, CHT])
        h1_hi, h1_lo = [sb(f"h1_{i}", [128, HP, HP], fp32r) for i in ("hi", "lo")]
        h2 = sb("h2", [128, 2, CHT])

        x1 = sb("x1", [PT, 2, PAIRS, C])
        xn = sb("xn", [PT, PAIRS, C])
        res1 = sb("res1", [PT, 2, PAIRS, C])
        res2 = sb("res2", [PT, 2, PAIRS, C])
        st = [sb(f"stats{i}", [PT, PAIRS, 6]) for i in range(2)]
        lnp = [sb(f"lnp{i}", [PT, 10, PAIRS]) for i in range(2)]
        xt = sb("xt", [C, WINS, 2, N])
        qt = sb("qt", [C, WINS, QROWS])
        km = sb("km", [C, WINS, 2, N])
        vb = sb("vb", [PT, 2, WINS, HEADS, D + 1])
        sc = sb("sc", [128, 2, QUADS, PAIRS, 2, N])
        mx = sb("mx", [128, 2, 2, PAIRS, 2])
        pt = sb("pt", [PT, PAIRS, QUADS, 2 * QROWS])
        rsum = sb("rsum", [128, PAIRS, HEADS])
        on = sb("on", [128, PAIRS, C])
        ot = sb("ot", [C, PAIRS, PT])
        x2 = sb("x2", [PT, PAIRS, C])
        z = sb("z", [PT, PAIRS, C])
        zt = sb("zt", [C, ST])
        g = sb("g", [128, HC, ST])
        y = sb("y", [PT, 2, PAIRS, C])

        bank = [ctx.enter_context(nc.psum_tensor(f"bank{i}", [128, 512], fp32)) for i in range(8)]
        RA, RB, RC = bank[4], bank[5:7], bank[7]
        A_JOBS = 3
        B_JOBS = 5
        SMALL = 6
        C_JOBS = 6

        conv_load, wload, prep, tb_store, tb_load = sem("conv_load"), sem("wload"), sem("prep"), sem("tb_store"), sem("tb_load")
        xc_in = [sem(f"xc_in{c}") for c in range(CHUNKS)]
        xc_out = [sem(f"xc_out{c}") for c in range(CHUNKS)]
        xct_ps = [sem(f"xct_ps{m}") for m in range(2)]
        xct_sb = [sem(f"xct_sb{m}") for m in range(2)]
        conv3_ps = [sem(f"conv3_ps{m}") for m in range(2)]
        xc_biased, xc_summed, xc_relu = sem("xc_biased"), sem("xc_summed"), sem("xc_relu")
        h1_split = sem("h1_split")
        conv1_ps, h1_sb, conv2_ps, h2_sb = sem("conv1_ps"), sem("h1_sb"), sem("conv2_ps"), sem("h2_sb")
        biasm_done = sem("biasm_done")
        x1_in = [sem(f"x1_in{u}") for u in range(2)]
        y_out = [sem(f"y_out{u}") for u in range(2)]
        stats = [sem(f"stats_sem{i}") for i in range(2)]
        small = [sem(f"small{i}") for i in range(2)]
        xn_sb, z_sb, res1_sb, res2_sb = sem("xn_sb"), sem("z_sb"), sem("res1_sb"), sem("res2_sb")
        a_full, a_out, c_full, c_out = sem("a_full"), sem("a_out"), sem("c_full"), sem("c_out")
        b_full = [sem(f"b_full{j}") for j in range(2)]
        b_out = [sem(f"b_out{j}") for j in range(2)]
        s_full, s_out, max_done, sub_done, exp_done = [sem(n) for n in
                                                       ("s_full", "s_out", "max_done", "sub_done", "exp_done")]
        rsum_done = sem("rsum_done")

        CONV_LOADS, LOADS = [], []

        def b_before(t, job):
            if job == 0:
                return B_JOBS * t.n - (B_JOBS - 1)
            return B_JOBS * t.n + job + (1 if t.back(-1).there() else 0)

        def y_stored(u, n):
            return 16 * MOVES * n + (16 * MOVES * (WIN - 1) * (n // (STRIPS // 2)) if u else 0)

        block_ = ctx.enter_context(nc.Block())

        def at(e, name):
            wait(e, prep, PREP.index(name))

        @block_.sync
        def _(sp):
            def conv_load_in(dst, src):
                CONV_LOADS.append(dst)
                sp.dma_start(dst, src).then_inc(conv_load, 16)

            def load(dst, src):
                LOADS.append(dst)
                sp.dma_start(dst, src).then_inc(wload, 16)

            def everywhere(name, parts, n=C):
                return bass.AP(tensor=a[name].tensor, offset=0, ap=[[0, parts], [1, n]])

            def column(name):
                return a[name].rearrange("(p o) -> p o", o=1)

            def chunk(dram, gp, c, m):
                return dram[2 * gp + m, ROWS * c:ROWS * c + ROWS].rearrange("(t r) w ch -> (r w) t ch", t=TILES)

            def chunk_in(gp, c):
                for m in range(2):
                    sp.dma_start(xc[:, c, m], chunk(a["x"], gp, c, m)).then_inc(xc_in[c], 16)

            def chunk_out(gp, c):
                sp.wait_ge(xc_relu, 2 * (CHUNKS * gp + c + 1))
                for m in range(2):
                    sp.dma_start(chunk(x1_dram, gp, c, m), xc[:, c, m]).then_inc(xc_out[c], 16)
                    if c == 0:
                        sp.dma_start(x1_dram[2 * gp + m, H:H + 2].rearrange("r w c -> (r w) c"),
                                     xc[:, 0, m, 0, :]).then_inc(xc_out[0], 16)
                        sp.dma_start(x1_dram[2 * gp + m, H + 2], xc[0:W, 0, m, 1, :]).then_inc(xc_out[0], 16)

            def twice(name):
                return bass.AP(tensor=a[name].tensor, offset=0, ap=[[0, 2], [1, MID], [1, 1]])

            for i, nm in enumerate("vgmb"):
                for l in range(2):
                    conv_load_in(bn[:, "gbmv".index(nm), l:l + 1], twice(f"{nm}{l + 1}"))
                conv_load_in(b3[:, "gbmv".index(nm), :], everywhere(f"{nm}3", 128))
            conv_load_in(w3[:], bass.AP(tensor=a["w3"].tensor, offset=0, ap=[[0, 2], [C, MID], [1, C]]))
            conv_load_in(groupmask[:], a["groupmask"].rearrange("p (m o) -> p m o", m=2))
            for t in range(TAPS):
                conv_load_in(w2raw[:, t, :], bass.AP(tensor=a["w2"].tensor, offset=t * 2 * MID,
                                                     ap=[[0, MID], [MID, 2], [1, MID]]))
            conv_load_in(w1[:], a["w1"])
            conv_load_in(ident[:], a["ident"])
            for c in range(CHUNKS):
                chunk_in(0, c)
            load(headmask[:], a["headmask"])
            load(vmask[:], a["vmask"].rearrange("p (h d) -> p h d", h=HEADS))
            load(winmask[:].rearrange("p a k m -> p (a k m)"), a["winmask"])
            load(wqkv[:], a["qkv_wT"])
            load(wproj[:], a["proj_wT"])
            load(fc1[:], a["fc1_wT"])
            load(fc2[:], a["fc2_wT"].rearrange("(c p) n -> p c n", p=128))
            with nc.allow_non_contiguous_dma(reason="a few hundred elements, once"):
                load(fc1b[:], a["fc1_b"].rearrange("(c p) -> p c", p=128))
                load(cpbb1[:], a["cpb_b1"].rearrange("(c p) -> p c", p=128))
            load(projb[:], everywhere("proj_b", PT))
            load(fc2b[:], everywhere("fc2_b", PT))
            for i, nm in enumerate(("norm1_w", "norm1_b", "norm2_w", "norm2_b")):
                load(ln[:, i:i + 1], column(nm))
            load(coords[:], a["coords"])
            load(cpbw1[:], a["cpb_w1T"])
            load(cpbw2[:], a["cpb_w2T"].rearrange("(c p) n -> p c n", p=128))
            for i, nm in enumerate(("h_times", "ws_scalar", "ws_scalar2", "pow_para")):
                load(par[:, i:i + 1], everywhere(nm, 2, 1))

            def spread_bias(nj):
                for v in range(2):
                    for ni in range(WIN):
                        first = REL - 1 - ((nj + WIN - 1) * (2 * WIN - 1) + ni + WIN - 1)
                        src = bass.AP(tensor=tb_dram.tensor, offset=first,
                                      ap=[[REL, HEADS], [2 * WIN - 1, WIN], [1, WIN]])
                        n = v * QROWS + nj * WIN + ni
                        sp.dma_start(relb[n:n + 1], src).then_inc(tb_load, 16)

            def chunks(gp, c):
                if c < CHUNKS:
                    chunk_out(gp, c)
                if c >= 2:
                    sp.wait_ge(xc_out[c - 2], (32 if c > 2 else 96) * (gp + 1))
                    chunk_in(gp + 1, c - 2)

            for c in range(CHUNKS + 2):
                chunks(0, c)
            sp.wait_ge(prep, PREP.index("table") + 1)
            sp.dma_start(tb_dram, tb[:]).then_inc(tb_store, 16)
            sp.wait_ge(tb_store, 16)
            for c in range(CHUNKS + 2):
                chunks(1, c)
                if c < WIN:
                    spread_bias(c)
            with sp.Fori(2, BPAIRS - 1) as gp:
                for c in range(CHUNKS + 2):
                    chunks(gp, c)
            for c in range(CHUNKS):
                chunk_out(BPAIRS - 1, c)
            for c in range(CHUNKS):
                sp.wait_ge(xc_out[c], (32 if c else 96) * BPAIRS)

            def columns(p):
                c0 = 2 * WIN * p + SHIFT
                if p < PAIRS - 1:
                    return [(c0, 0, 2 * WIN)]
                return [(c0, 0, W - c0), (0, W - c0, 2 * WIN - (W - c0))]

            def block(dram, img, r, c, nj):
                d = dram[img, bass.ds(r, WIN), c:c + nj, :]
                return d.rearrange("i j c -> j i c")

            def load_strip(img, s, u):
                n = STRIPS * img + s
                wait(sp, xn_sb, n - 1)
                wait(sp, res1_sb, n - 1)
                for p in range(PAIRS):
                    for c, j0, nj in columns(p):
                        sp.dma_start(x1[WIN * j0:WIN * (j0 + nj), u, p, :],
                                     block(x1_dram, img, WIN * s + SHIFT, c, nj)).then_inc(x1_in[u], 16)

            def store_strip(img, s, u, last=False):
                sp.wait_ge(c_out, C_JOBS * (STRIPS * img + s + 1))
                for p in range(PAIRS):
                    for c, j0, nj in columns(p):
                        if not last:
                            sp.dma_start(block(out, img, WIN * s + SHIFT, c, nj),
                                         y[WIN * j0:WIN * (j0 + nj), u, p, :]).then_inc(y_out[u], 16)
                            continue
                        for i in range(WIN):
                            rows = y[WIN * j0 + i:WIN * (j0 + nj - 1) + i + 1:WIN, u, p, :]
                            sp.dma_start(out[img, (WIN * s + SHIFT + i) % H, c:c + nj, :], rows).then_inc(y_out[u], 16)

            for s in range(LEAD):
                load_strip(0, s, s % 2)
            with sp.Fori(0, B - 1) as img:
                for s in range(STRIPS):
                    if s + LEAD < STRIPS:
                        load_strip(img, s + LEAD, (s + LEAD) % 2)
                    else:
                        load_strip(img + 1, s + LEAD - STRIPS, (s + LEAD) % 2)
                    store_strip(img, s, s % 2, s == STRIPS - 1)
            for s in range(STRIPS):
                if s + LEAD < STRIPS:
                    load_strip(B - 1, s + LEAD, (s + LEAD) % 2)
                store_strip(B - 1, s, s % 2, s == STRIPS - 1)
            for u in range(2):
                sp.wait_ge(y_out[u], y_stored(u, NS // 2))

        @block_.tensor
        def _(pe):
            def bias_steps(c):
                if c == 6:
                    at(pe, "hidden_ps")
                    for i in range(CPB // 128):
                        mm = nc.tensor.matmul(bank[6][:, REL * i:REL * i + REL], cpbw1[:, 128 * i:128 * i + 128],
                                              tab[:], start=True, stop=True)
                    mm.then_inc(prep, 1)
                if c == 7:
                    at(pe, "table_ps")
                    for i in range(CPB // 128):
                        mm = nc.tensor.matmul(bank[7][0:HEADS, 0:REL], cpbw2[:, i, :], hid[:, i, :],
                                              start=i == 0, stop=i == CPB // 128 - 1)
                    mm.then_inc(prep, 1)

            pe.wait_ge(conv_load, 16 * len(CONV_LOADS))
            pe.wait_ge(prep, len(CONV_PREP))

            def x_to_channels(gp, c):
                n = CHUNKS * gp + c
                pe.wait_ge(xc_in[c], 32 * (gp + 1))
                for m in range(2):
                    wait(pe, xct_sb[m], n)
                    for t in range(TILES):
                        mm = nc.tensor.transpose(bank[m][:, CT * t:CT * t + CT], xc[:, c, m, t, :],
                                                 ident[0:CT, 0:CT])
                    mm.then_inc(xct_ps[m], 1)

            def conv1(gp, c):
                n = CHUNKS * gp + c
                wait(pe, h1_sb, n)
                for m in range(2):
                    pe.wait_ge(xct_sb[m], n + 1)
                    mm = nc.tensor.matmul(bank[2][MID * m:MID * m + MID, 0:CHT], w1[:], xct[:, m, :],
                                          start=True, stop=True)
                mm.then_inc(conv1_ps, 1)

            def conv2(gp, c):
                n = CHUNKS * gp + c
                pe.wait_ge(h1_split, n + (2 if c < CHUNKS - 1 else 1))
                wait(pe, h2_sb, n)
                parts = ((w2_hi, h1_hi), (w2_hi, h1_lo), (w2_lo, h1_hi))
                for t in range(TAPS):
                    dy, dx = divmod(t, 3)
                    for k, (w_part, h_part) in enumerate(parts):
                        mm = nc.tensor.matmul(bank[3][:, 0:CHT], w_part[:, t],
                                              h_part[:, ROWS * c + dy:ROWS * c + dy + ROWS, dx:dx + W],
                                              start=t == 0 and k == 0, stop=t == TAPS - 1 and k == len(parts) - 1)
                mm.then_inc(conv2_ps, 1)

            def conv3(gp, c):
                n = CHUNKS * gp + c
                pe.wait_ge(h2_sb, n + 1)
                wait(pe, xc_summed, 2 * n)
                for m in range(2):
                    for t in range(TILES):
                        mm = nc.tensor.matmul(bank[4 + m][0:CT, C * t:C * t + C],
                                              h2[MID * m:MID * m + MID, c % 2, CT * t:CT * t + CT],
                                              w3[MID * m:MID * m + MID, :], start=True, stop=True)
                    mm.then_inc(conv3_ps[m], 1)

            def convs(gp, c):
                if c == 0:
                    x_to_channels(gp, 0)
                if c < CHUNKS:
                    conv1(gp, c)
                if c + 1 < CHUNKS:
                    x_to_channels(gp, c + 1)
                if c >= 2:
                    conv3(gp, c - 2)
                if 1 <= c <= CHUNKS:
                    conv2(gp, c - 1)

            over_chunks(pe, convs, bias_steps)
            pe.wait_ge(h2_sb, CHUNKS * BPAIRS)
            pe.wait_ge(xc_summed, 2 * CHUNKS * BPAIRS)

            def to_channels(ring, src, full):
                for p in range(PAIRS):
                    mm = nc.tensor.transpose(ring[:, PT * p:PT * p + PT], src[:, p, :], ident[0:PT, 0:PT])
                mm.then_inc(full, 1)

            def values(t, j):
                wait(pe, b_out[j], b_before(t, 0))
                for w in range(4):
                    rows = xt[:, 4 * j + w].rearrange("c v n -> c (v n)")
                    mm = nc.tensor.matmul(RB[j][0:PT, C * w:C * w + C], rows, wqkv[:, 2 * C:3 * C],
                                          start=True, stop=True)
                mm.then_inc(b_full[j], 1)

            def project(t, i):
                wait(pe, a_out, A_JOBS * t.n + 1 + i)
                nc.tensor.matmul(RA[:, 0:ST], wqkv[:, C * i:C * i + C], xt[:, :, 0, :],
                                 start=True, stop=True).then_inc(a_full, 1)

            def scores(t, r, i):
                pe.wait_ge(a_out, A_JOBS * t.n + 3)
                wait(pe, s_out, QUADS * (t.n - 1) + 2 * r + 2)
                for w in range(4 * i, 4 * i + 4):
                    p, v = divmod(w, 2)
                    for q in (2 * r, 2 * r + 1):
                        mm = nc.tensor.matmul(bank[q][QROWS * v:QROWS * v + QROWS, 2 * N * p:2 * N * p + 2 * N],
                                              qt[32 * q:32 * q + 32, w],
                                              km[32 * q:32 * q + 32, w].rearrange("p h m -> p (h m)"),
                                              start=True, stop=True)
                if i == 1:
                    mm.then_inc(s_full, 1)

            def probs_t(t, j):
                if j == 0:
                    pe.wait_ge(exp_done, t.n + 1)
                wait(pe, b_out[j % 2], b_before(t, 1 + j // 2))
                for q in range(QUADS):
                    mm = nc.tensor.transpose(RB[j % 2][0:PT, 128 * q:128 * q + 128],
                                             sc[:, t.u, q, j].rearrange("p h m -> p (h m)"), ident[:])
                mm.then_inc(b_full[j % 2], 1)

            def attend(t, j):
                for i in range(2):
                    wait(pe, b_out[i], b_before(t, 3 if i == j or j == 1 else 2))
                o = RB[j][:, 0:2 * HEADS * (D + 1)].rearrange("p (k q n) -> p k q n", k=2, q=QUADS)
                for k in range(2):
                    for v in range(2):
                        w = 2 * (2 * j + k) + v
                        for q in range(QUADS):
                            mm = nc.tensor.matmul(o[QROWS * v:QROWS * v + QROWS, k, q],
                                                  pt[:, 2 * j + k, q, QROWS * v:QROWS * v + QROWS],
                                                  vb[:, t.u, w, 2 * q:2 * q + 2].rearrange("p h d -> p (h d)"),
                                                  start=True, stop=True)
                mm.then_inc(b_full[j], 1)

            def attention_out(t):
                wait(pe, b_out[0], b_before(t, 4))
                wait(pe, b_out[1], b_before(t, 4))
                for p in range(PAIRS):
                    mm = nc.tensor.transpose(RB[0][:, 128 * p:128 * p + 128], on[:, p, :], ident[:])
                mm.then_inc(b_full[0], 1)

            def projection(t):
                wait(pe, b_out[0], b_before(t, 5))
                for p in range(PAIRS):
                    mm = nc.tensor.matmul(RB[1][0:PT, C * p:C * p + C], ot[:, p, :], wproj[:],
                                          start=True, stop=True)
                mm.then_inc(b_full[1], 1)

            def hidden(t, j):
                wait(pe, c_out, C_JOBS * t.n + 1 + j)
                nc.tensor.matmul(RC[:, 0:ST], fc1[:, 128 * j:128 * j + 128], zt[:],
                                 start=True, stop=True).then_inc(c_full, 1)

            def mlp_out(t, pairs):
                wait(pe, c_out, C_JOBS * t.n + 5)
                for p in pairs:
                    for c in range(HC):
                        mm = nc.tensor.matmul(RC[0:PT, C * p:C * p + C], g[:, c, PT * p:PT * p + PT],
                                              fc2[:, c, :], start=c == 0, stop=c == HC - 1)
                if PAIRS - 1 in pairs:
                    mm.then_inc(c_full, 1)

            def strips(t):
                ahead, t1, t2, t3 = t.back(-1), t.back(1), t.back(2), t.back(3)
                if t.there():
                    pe.wait_ge(a_out, A_JOBS * t.n + 1)
                    project(t, 0)
                    values(t, 0)
                    project(t, 1)
                    values(t, 1)
                if t3.there():
                    hidden(t3, 0)
                if t.there():
                    scores(t, 0, 0)
                    scores(t, 0, 1)
                if t3.there():
                    hidden(t3, 1)
                if t.there():
                    scores(t, 1, 0)
                if t3.there():
                    hidden(t3, 2)
                if t.there():
                    scores(t, 1, 1)
                if t1.there():
                    probs_t(t1, 0)
                    probs_t(t1, 1)
                if t3.there():
                    hidden(t3, 3)
                if t1.there():
                    probs_t(t1, 2)
                    probs_t(t1, 3)
                    attend(t1, 0)
                if t3.there():
                    mlp_out(t3, (0, 1))
                if t1.there():
                    attend(t1, 1)
                if t3.there():
                    mlp_out(t3, (2,))
                if t1.there():
                    attention_out(t1)
                if ahead.there():
                    pe.wait_ge(xn_sb, ahead.n + 1)
                    wait(pe, a_out, A_JOBS * ahead.n)
                    to_channels(RA, xn, a_full)
                if t3.there():
                    mlp_out(t3, (3,))
                if t1.there():
                    projection(t1)
                if t2.there():
                    pe.wait_ge(z_sb, t2.n + 1)
                    wait(pe, c_out, C_JOBS * t2.n)
                    to_channels(RC, z, c_full)

            over_strips(pe, strips)

        @block_.scalar
        def _(act):
            def step(name, *args, **kw):
                at(act, name)
                nc.scalar.activation(*args, **kw).then_inc(prep, 1)

            def bias_steps(c):
                if c == 1:
                    act.wait_ge(wload, 16 * len(LOADS))
                    step("abs", par_abs[:, 0:3], par[:, 0:3], ACT.Abs)
                    at(act, "exp")
                    nc.scalar.activation(par_exp[:, 3:4], par[:, 3:4], ACT.Exp, scale=-1.0)
                    nc.scalar.activation(par_exp[:, 0:3], par_abs[:, 0:3], ACT.Exp, scale=-1.0).then_inc(prep, 1)
                    step("ln", par_ln[:, 0:3], par_exp[:, 0:3], ACT.Ln, bias=1.0)
                if c == 3:
                    step("magnitude", t_mag[:], t_prod[:], ACT.Abs)
                    step("sign", t_sign[:], t_prod[:], ACT.Sign)
                if c == 6:
                    at(act, "hidden")
                    for i in range(CPB // 128):
                        ins = nc.scalar.activation(hid[:, i, :], bank[6][:, REL * i:REL * i + REL], ACT.Relu,
                                                   bias=cpbb1[:, i:i + 1])
                    ins.then_inc(prep, 1)
                if c == 7:
                    step("table", tb[:], bank[7][0:HEADS, 0:REL], ACT.Copy)

            act.wait_ge(prep, len(CONV_PREP))

            def xct_out(gp, c):
                n = CHUNKS * gp + c
                act.wait_ge(xct_ps[0], n + 1)
                wait(act, conv1_ps, n)
                nc.scalar.activation(xct[:, 0, :], bank[0][:, 0:CHT], ACT.Copy).then_inc(xct_sb[0], 1)

            def h1_out(gp, c):
                n = CHUNKS * gp + c
                act.wait_ge(conv1_ps, n + 1)
                wait(act, h1_split, n - 1 if c else n)
                ps, norm = bank[2][:, 0:CHT], {"scale": bn_scale[:, 0:1], "bias": bn_bias[:, 0:1]}
                nc.scalar.activation(h1_hi[:, 1 + ROWS * c:1 + ROWS * c + ROWS, 1:1 + W],
                                     ps.rearrange("p (r w) -> p r w", w=W), ACT.Relu, **norm)
                nc.scalar.activation(h1[:, c % 2], ps, ACT.Relu, **norm).then_inc(h1_sb, 1)

            def h2_out(gp, c):
                n = CHUNKS * gp + c
                act.wait_ge(conv2_ps, n + 1)
                wait(act, conv3_ps[1], n if c == 0 else CHUNKS * gp + max(c - 1, 0))
                nc.scalar.activation(h2[:, c % 2, :], bank[3][:, 0:CHT], ACT.Relu,
                                     scale=bn_scale[:, 1:2], bias=bn_bias[:, 1:2]).then_inc(h2_sb, 1)

            def relu_out(gp, c):
                n = CHUNKS * gp + c
                for m in range(2):
                    act.wait_ge(xc_summed, 2 * n + m + 1)
                    nc.scalar.activation(xc[:, c, m], xc[:, c, m], ACT.Relu).then_inc(xc_relu, 1)

            def convs(gp, c):
                if c == 0:
                    xct_out(gp, 0)
                if c < CHUNKS:
                    h1_out(gp, c)
                if c + 1 < CHUNKS:
                    xct_out(gp, c + 1)
                if c >= 2:
                    relu_out(gp, c - 2)
                if 1 <= c <= CHUNKS:
                    h2_out(gp, c - 1)

            over_chunks(act, convs, bias_steps)

            def xt_out(t):
                act.wait_ge(a_full, A_JOBS * t.n + 1)
                for v in range(2):
                    i = nc.scalar.activation(xt[:, :, v, :], RA[:, 0:ST].rearrange("c (w n) -> c w n", n=N),
                                             ACT.Identity, scale=ln[:, 0:1], bias=ln[:, 1:2])
                i.then_inc(a_out, 1)

            def q_out(t):
                act.wait_ge(a_full, A_JOBS * t.n + 2)
                wait(act, s_full, 2 * t.n)
                nc.scalar.activation(qt[:, :, 0:N], RA[:, 0:ST].rearrange("c (w n) -> c w n", n=N),
                                     ACT.Copy).then_inc(a_out, 1)

            def k_out(t):
                act.wait_ge(a_full, A_JOBS * t.n + 3)
                for hh in range(2):
                    i = nc.scalar.activation(km[:, :, hh, :], RA[:, 0:ST].rearrange("c (w n) -> c w n", n=N),
                                             ACT.Identity, scale=headmask[:, hh:hh + 1])
                i.then_inc(a_out, 1)

            def zt_out(t):
                act.wait_ge(c_full, C_JOBS * t.n + 1)
                nc.scalar.activation(zt[:], RC[:, 0:ST], ACT.Identity, scale=ln[:, 2:3],
                                     bias=ln[:, 3:4]).then_inc(c_out, 1)

            def gelu(t, j):
                act.wait_ge(c_full, C_JOBS * t.n + 2 + j)
                nc.scalar.activation(g[:, j, :], RC[:, 0:ST], ACT.Gelu, bias=fc1b[:, j:j + 1]).then_inc(c_out, 1)

            def pt_out(t, j):
                act.wait_ge(b_full[j % 2], b_before(t, 1 + j // 2) + 1)
                nc.scalar.activation(pt[:, j].rearrange("p q n -> p (q n)"), RB[j % 2][0:PT, :],
                                     ACT.Copy).then_inc(b_out[j % 2], 1)

            def ot_out(t):
                act.wait_ge(b_full[0], b_before(t, 4) + 1)
                wait(act, b_full[1], b_before(t, 4))
                nc.scalar.activation(ot[:].rearrange("c p (v n) -> c (p v) n", v=2),
                                     RB[0][:].rearrange("c (w n) -> c w n", n=64)[:, :, 0:N],
                                     ACT.Copy).then_inc(b_out[0], 1)

            def exponentials(t):
                for r in range(2):
                    act.wait_ge(sub_done, 2 * t.n + r + 1)
                    half_sc = sc[:, t.u, 2 * r:2 * r + 2].rearrange("p q k h m -> p (q k h m)")
                    i = nc.scalar.activation(half_sc, half_sc, ACT.Exp)
                i.then_inc(exp_done, 1)

            def strips(t):
                ahead, t1, t2, t3 = t.back(-1), t.back(1), t.back(2), t.back(3)
                if t.there():
                    q_out(t)
                    k_out(t)
                if t3.there():
                    gelu(t3, 0)
                    gelu(t3, 1)
                    gelu(t3, 2)
                if t1.there():
                    pt_out(t1, 0)
                    pt_out(t1, 1)
                if t3.there():
                    gelu(t3, 3)
                if t1.there():
                    pt_out(t1, 2)
                    pt_out(t1, 3)
                if t.there():
                    exponentials(t)
                if t1.there():
                    ot_out(t1)
                if ahead.there():
                    xt_out(ahead)
                if t2.there():
                    zt_out(t2)

            over_strips(act, strips)

        def norm_stats(i, t, src):
            for p in range(PAIRS):
                ins = nc.vector.bn_stats(st[i][:, p, :], src[:, p, :])
            ins.then_inc(stats[i], 1)

        @block_.vector
        def _(dve):
            def step(name, f, *args, **kw):
                at(dve, name)
                f(*args, **kw).then_inc(prep, 1)

            V = nc.vector
            at(dve, "border")
            V.memset(h1_hi[:].bitcast(fp32), 0.0)
            V.memset(h1_lo[:].bitcast(fp32), 0.0).then_inc(prep, 1)
            at(dve, "w2")
            for t in range(TAPS):
                i = V.tensor_tensor(out=w2[:, t], in0=w2raw[:, t].unsqueeze(1).to_broadcast([128, 2, MID]),
                                    in1=groupmask[:], op=ALU.mult)
            i.then_inc(prep, 1)
            w2_flat = w2[:].rearrange("p t m o -> p t (m o)")
            step("w2_hi", V.tensor_copy, w2_hi[:], w2_flat)
            step("w2_lo", V.tensor_tensor, out=w2_lo[:], in0=w2_flat, in1=w2_hi[:].bitcast(fp32), op=ALU.subtract)

            def bias_steps(c):
                if c == 2:
                    step("positive", V.tensor_scalar, par_pos[:, 0:3], par[:, 0:3], 0.0, None, ALU.max)
                    step("softplus", V.tensor_tensor, out=par_sp[:, 0:3], in0=par_pos[:, 0:3], in1=par_ln[:, 0:3],
                         op=ALU.add)
                    step("denominator", V.tensor_scalar, sig_den[:], par_exp[:, 3:4], 1.0, None, ALU.add)
                    step("sigmoid", V.reciprocal, sig[:], sig_den[:])
                    step("recip", V.reciprocal, ws2_recip[:], par_sp[:, 2:3])
                    step("product", V.tensor_scalar, t_prod[:], coords[:], par_sp[:, 0:1], None, ALU.mult)
                if c == 4:
                    step("scaled", V.tensor_scalar, t_scaled[:], t_mag[:], par_sp[:, 1:2], 1e-6, ALU.mult, ALU.add)
                    step("exponent", V.tensor_copy, t_exp[:], sig[:].to_broadcast([2, REL]))
                if c == 5:
                    step("signed", V.tensor_tensor, out=t_signed[:], in0=t_sign[:], in1=t_pow[:], op=ALU.mult)
                    step("tab", V.tensor_scalar, tab[:], t_signed[:], ws2_recip[:], None, ALU.mult)
                if c == 8:
                    at(dve, "ones")
                    for u in range(2):
                        i = V.tensor_copy(vb[:, u, :, :, D],
                                          vmask[:, :, 0].unsqueeze(1).to_broadcast([PT, WINS, HEADS]))
                    i.then_inc(prep, 1)

            dve.wait_ge(prep, len(CONV_PREP))

            def xct_out(gp, c):
                n = CHUNKS * gp + c
                dve.wait_ge(xct_ps[1], n + 1)
                wait(dve, conv1_ps, n)
                V.tensor_copy(xct[:, 1, :], bank[1][:, 0:CHT]).then_inc(xct_sb[1], 1)

            def h1_rest(gp, c):
                dve.wait_ge(h1_sb, CHUNKS * gp + c + 1)
                rows, cols = slice(1 + ROWS * c, 1 + ROWS * c + ROWS), slice(1, 1 + W)
                V.tensor_tensor(out=h1_lo[:, rows, cols], in0=h1[:, c % 2].rearrange("p (r w) -> p r w", w=W),
                                in1=h1_hi[:, rows, cols].bitcast(fp32), op=ALU.subtract).then_inc(h1_split, 1)

            def sum_out(gp, c):
                n = CHUNKS * gp + c
                dve.wait_ge(xc_biased, n + 1)
                for m in range(2):
                    dve.wait_ge(conv3_ps[m], n + 1)
                    x_m = xc[:, c, m].rearrange("p t c -> p (t c)")
                    V.tensor_tensor(out=x_m, in0=bank[4 + m][0:CT, :], in1=x_m, op=ALU.add).then_inc(xc_summed, 1)

            def convs(gp, c):
                if c == 0:
                    xct_out(gp, 0)
                if c + 1 < CHUNKS:
                    xct_out(gp, c + 1)
                if c < CHUNKS:
                    h1_rest(gp, c)
                if c >= 2:
                    sum_out(gp, c - 2)

            over_chunks(dve, convs, bias_steps)

            dve.wait_ge(tb_load, 16 * PT)
            for kind in range(2):
                for h in range(HEADS):
                    i = V.tensor_tensor(out=biasm[:, kind, h // 2, :, h % 2, :], in0=winmask[:, kind],
                                        in1=relb[:, h].unsqueeze(1).to_broadcast([128, PAIRS, N]), op=ALU.add)
            i.then_inc(biasm_done, 1)
            dve.wait_ge(biasm_done, 1)

            def v_out(t, j):
                dve.wait_ge(b_full[j], b_before(t, 0) + 1 if t.c or not t.fixed else 1)
                V.tensor_tensor(out=vb[:, t.u, 4 * j:4 * j + 4, :, 0:D],
                                in0=RB[j][0:PT, :].rearrange("p (w h d) -> p w h d", w=4, h=HEADS),
                                in1=vmask[:].unsqueeze(1).to_broadcast([PT, 4, HEADS, D]),
                                op=ALU.mult).then_inc(b_out[j], 1)

            def biased(t):
                for q in range(QUADS):
                    dve.wait_ge(s_full, 2 * t.n + q // 2 + 1)
                    if t.u == 0:
                        b = biasm[:, 0, q]
                    elif t.fixed:
                        b = biasm[:, int(t.n % STRIPS == STRIPS - 1), q]
                    else:
                        b = biasm[:, bass.ds((t.half % (STRIPS // 2)) // (STRIPS // 2 - 1), 1), q]
                        b = b.rearrange("p o k h m -> p (o k) h m")
                    V.tensor_tensor(out=sc[:, t.u, q].rearrange("p k h m -> p (k h m)"), in0=bank[q][:, 0:ST],
                                    in1=b.rearrange("p k h m -> p (k h m)"), op=ALU.add).then_inc(s_out, 1)

            def maxima(t):
                wait(dve, sub_done, 2 * t.n)
                for r in range(2):
                    dve.wait_ge(s_out, QUADS * t.n + 2 * r + 2)
                    V.reduce_max(mx[:, r].rearrange("p q k h -> p (q k h)"),
                                 sc[:, t.u, 2 * r:2 * r + 2].rearrange("p q k h m -> p (q k h) m"),
                                 AX.X).then_inc(max_done, 1)

            def normalise(t, j):
                dve.wait_ge(b_full[j], b_before(t, 3) + 1)
                wait(dve, b_full[0], b_before(t.back(1), 5) if not (t.fixed and t.c == 0) else 0)
                o = RB[j][:, 0:2 * HEADS * (D + 1)].rearrange("p (k h d) -> p k h d", k=2, h=HEADS)
                V.reciprocal(rsum[:, 2 * j:2 * j + 2, :], o[:, :, :, D]).then_inc(rsum_done, 1)
                dve.wait_ge(rsum_done, 2 * t.n + j + 1)
                V.tensor_tensor(out=on[:, 2 * j:2 * j + 2, :].rearrange("p k (h d) -> p k h d", h=HEADS),
                                in0=o[:, :, :, 0:D],
                                in1=rsum[:, 2 * j:2 * j + 2, :].unsqueeze(3).to_broadcast([128, 2, HEADS, D]),
                                op=ALU.mult).then_inc(b_out[j], 1)

            def x1_stats(t):
                dve.wait_ge(x1_in[t.u], 16 * MOVES * (t.half + 1))
                wait(dve, small[0], SMALL * t.n)
                norm_stats(0, t, x1[:, t.u])

            def norm(i, t, src, dst, done):
                dve.wait_ge(small[i], SMALL * t.n + SMALL)
                for p in range(PAIRS):
                    ins = V.tensor_scalar(dst[:, p, :], src[:, p, :], lnp[i][:, 8, p:p + 1], lnp[i][:, 9, p:p + 1],
                                          ALU.mult, ALU.add)
                ins.then_inc(done, 1)

            def x1_norm(t):
                wait(dve, a_full, A_JOBS * (t.n - 1) + 1)
                norm(0, t, x1[:, t.u], xn, xn_sb)

            def x2_norm(t):
                wait(dve, c_full, C_JOBS * (t.n - 1) + 1)
                norm(1, t, x2, z, z_sb)

            def x2_out(t):
                dve.wait_ge(b_full[1], b_before(t, 4) + 1)
                dve.wait_ge(res1_sb, t.n + 1)
                wait(dve, res2_sb, t.n)
                V.tensor_tensor(out=x2[:].rearrange("p k c -> p (k c)"), in0=RB[1][0:PT, :],
                                in1=res1[:, t.u].rearrange("p k c -> p (k c)"), op=ALU.add).then_inc(b_out[1], 1)
                dve.wait_ge(b_out[1], b_before(t, 5))
                norm_stats(1, t, x2)

            def y_sum(t):
                dve.wait_ge(c_full, C_JOBS * t.n + 6)
                wait(dve, y_out[t.u], y_stored(t.u, t.half))
                dve.wait_ge(res2_sb, t.n + 1)
                V.tensor_tensor(out=y[:, t.u].rearrange("p k c -> p (k c)"), in0=RC[0:PT, :],
                                in1=res2[:, t.u].rearrange("p k c -> p (k c)"), op=ALU.add).then_inc(c_out, 1)

            def strips(t):
                ahead, t1, t2, t3 = t.back(-1), t.back(1), t.back(2), t.back(3)
                if t.there():
                    v_out(t, 0)
                if ahead.there():
                    x1_stats(ahead)
                if t.there():
                    v_out(t, 1)
                if t2.there():
                    x2_norm(t2)
                if ahead.there():
                    x1_norm(ahead)
                if t.there():
                    biased(t)
                    maxima(t)
                if t1.there():
                    normalise(t1, 0)
                    normalise(t1, 1)
                if t3.there():
                    y_sum(t3)
                if t1.there():
                    x2_out(t1)

            over_strips(dve, strips)

        @block_.gpsimd
        def _(pool):
            P = nc.gpsimd

            def step(name, f, *args, **kw):
                at(pool, name)
                f(*args, **kw).then_inc(prep, 1)

            def tt(o, x, y_, op):
                return P.tensor_tensor(out=o, in0=x, in1=y_, op=op)

            step("half", P.memset, half[:], -0.5)
            step("quarter", P.memset, quarter[:], 0.25)
            step("relb_clear", P.memset, relb[:], 0.0)
            step("qt_clear", P.memset, qt[:], 0.0)
            pool.wait_ge(conv_load, 16 * len(CONV_LOADS))
            for n, v, shift_, rstd_, scale_, bias_, q in (
                    ("bn", bn, bn_shift, bn_rstd, bn_scale, bn_bias, bn_var),
                    ("b3", b3, b3_shift, b3_rstd, b3_scale, b3_bias, b3_var)):
                step(f"{n}_var", P.tensor_scalar, q[:], v[:, 3], BN_EPS, None, ALU.add)
                step(f"{n}_rstd", tt, rstd_[:], q[:], half[:, 0:q.shape[1]], ALU.pow)
                step(f"{n}_scale", tt, scale_[:], v[:, 0], rstd_[:], ALU.mult)
                step(f"{n}_shift", tt, shift_[:], v[:, 2], scale_[:], ALU.mult)
                step(f"{n}_bias", tt, bias_[:], v[:, 1], shift_[:], ALU.subtract)
            step("w3", tt, w3[:], w3[:], b3_scale[:], ALU.mult)

            def convs(gp, c):
                if c < CHUNKS:
                    n = CHUNKS * gp + c
                    pool.wait_ge(xct_ps[1], n + 1)
                    x_c = xc[:, c].rearrange("p m t c -> p (m t) c")
                    P.tensor_tensor(out=x_c, in0=x_c, in1=b3_bias[0:CT].unsqueeze(1).to_broadcast(
                        [CT, 2 * TILES, C]), op=ALU.add).then_inc(xc_biased, 1)

            def bias_steps(c):
                if c == 4:
                    step("power", tt, t_pow[:], t_scaled[:], t_exp[:], ALU.pow)

            pool.wait_ge(prep, len(CONV_PREP))
            over_chunks(pool, convs, bias_steps)
            pool.wait_ge(prep, len(PREP))

            def factors(i, t, x):
                _, mean_e, dev_e, _, mean_o, dev_o = [st[i][:, :, k] for k in range(6)]
                sum_, dif, dev, dif2, dev_eps, dif4, var, negm, rstd, shift = [lnp[i][:, k] for k in range(10)]
                pool.wait_ge(stats[i], t.n + 1)
                tt(sum_, mean_e, mean_o, ALU.add)
                tt(dif, mean_e, mean_o, ALU.subtract)
                tt(dev, dev_e, dev_o, ALU.add).then_inc(small[i], 1)
                pool.wait_ge(small[i], SMALL * t.n + 1)
                tt(dif2, dif, dif, ALU.mult)
                P.tensor_scalar(dev_eps, dev, 1.0 / C, LN_EPS, ALU.mult, ALU.add)
                tt(negm, sum_, half[0:PT, 0:PAIRS], ALU.mult).then_inc(small[i], 1)
                pool.wait_ge(small[i], SMALL * t.n + 2)
                tt(dif4, dif2, quarter[:], ALU.mult).then_inc(small[i], 1)
                pool.wait_ge(small[i], SMALL * t.n + 3)
                tt(var, dif4, dev_eps, ALU.add).then_inc(small[i], 1)
                pool.wait_ge(small[i], SMALL * t.n + 4)
                wait(pool, x, t.n)
                tt(rstd, var, half[0:PT, 0:PAIRS], ALU.pow).then_inc(small[i], 1)
                pool.wait_ge(small[i], SMALL * t.n + 5)
                tt(shift, negm, rstd, ALU.mult).then_inc(small[i], 1)

            def add_bias(res, src, bias, done):
                P.tensor_tensor(out=res, in0=src, in1=bias[:].unsqueeze(1).to_broadcast([PT, PAIRS, C]),
                                op=ALU.add).then_inc(done, 1)

            def residual1(t):
                pool.wait_ge(stats[0], t.n + 1)
                wait(pool, b_out[1], b_before(t.back(2), 5) if t.back(2).there() else 0)
                add_bias(res1[:, t.u], x1[:, t.u], projb, res1_sb)

            def residual2(t):
                pool.wait_ge(b_out[1], b_before(t, 5))
                wait(pool, c_out, C_JOBS * (t.n - 1))
                add_bias(res2[:, t.u], x2[:], fc2b, res2_sb)

            def subtract(t):
                for r in range(2):
                    pool.wait_ge(max_done, 2 * t.n + r + 1)
                    s_r = sc[:, t.u, 2 * r:2 * r + 2].rearrange("p q k h m -> p (q k h) m")
                    m_r = mx[:, r].rearrange("p q k h -> p (q k h)").unsqueeze(2)
                    P.tensor_tensor(out=s_r, in0=s_r, in1=m_r.to_broadcast([128, 2 * HEADS, N]),
                                    op=ALU.subtract).then_inc(sub_done, 1)

            def strips(t):
                ahead, t2 = t.back(-1), t.back(2)
                if t2.there():
                    factors(1, t2, z_sb)
                if ahead.there():
                    factors(0, ahead, xn_sb)
                if t2.there():
                    residual2(t2)
                if t.there():
                    subtract(t)
                if ahead.there():
                    residual1(ahead)

            over_strips(pool, strips)


_OUT = (B, H, W, C)


def kernel(**inputs):
    import concourse.bacc as bacc
    from concourse.bass_utils import run_bass_kernel_spmd as run

    def arr(name):
        return np.ascontiguousarray(inputs[name])

    arrays = {"x": arr("x")}
    for i in "123":
        for v in "gbmv":
            arrays[v + i] = arr(f"L0_conv_{v}{i}")
    arrays["w1"] = arr("L0_conv_w1").reshape(C, MID)
    arrays["w2"] = arr("L0_conv_w2").reshape(-1)
    arrays["w3"] = arr("L0_conv_w3").reshape(MID, C)
    for v in ("norm1_w", "norm1_b", "norm2_w", "norm2_b", "proj_b", "fc1_b", "fc2_b", "cpb_b1"):
        arrays[v] = arr("L1_conv_" + v)
    for v in ("h_times", "pow_para", "ws_scalar", "ws_scalar2"):
        arrays[v] = arr("L1_conv_" + v).reshape(1)
    for v in ("qkv_w", "proj_w", "fc1_w", "fc2_w", "cpb_w1", "cpb_w2"):
        arrays[v + "T"] = np.ascontiguousarray(arr("L1_conv_" + v).T)
    arrays.update(shape_constants())

    nc = bacc.Bacc("TRN2", target_bir_lowering=False, num_devices=1)
    handles = {n: nc.dram_tensor("in_" + n, v.shape, mybir.dt.float32, kind="ExternalInput").ap()
               for n, v in arrays.items()}
    out = nc.dram_tensor("out_x", _OUT, mybir.dt.float32, kind="ExternalOutput").ap()
    program(nc, handles, out)
    r = run(nc, [{"in_" + n: v for n, v in arrays.items()}], core_ids=[0])
    return r.results[0]["out_x"]
```

```python
import numpy as np
from collections import namedtuple
from contextlib import ExitStack

import concourse.bass as bass
from concourse import mybir

B, H, W, C = 32, 56, 56, 128
MID = 64
TAPS = 9
HEADS, D = 8, 16
WIN, SHIFT = 7, 3
N = WIN * WIN
STRIPS = H // WIN
WINS = W // WIN
PAIRS = WINS // 2
PT = 2 * N
ST = WINS * N
NS = B * STRIPS
QUADS = 4
QROWS = 64
HID = 4 * C
HC = HID // 128
REL = (2 * WIN - 1) ** 2
CPB = 256
BN_EPS, LN_EPS = 1e-3, 1e-5
NEG = -1e9

ROWS = 8
CHUNKS = H // ROWS
CT = 2 * W
TILES = ROWS * W // CT
CHT = ROWS * W
HP = W + 2
BPAIRS = B // 2

LEAD = 5
MOVES = PAIRS + 1


def shape_constants():
    c = {}
    c["ident"] = np.eye(128, dtype=np.float32)
    g = np.arange(-(WIN - 1), WIN, dtype=np.float32) / np.float32(WIN - 1)
    grid = np.stack([np.tile(g, 2 * WIN - 1), np.repeat(g, 2 * WIN - 1)], 0)
    c["coords"] = np.ascontiguousarray(grid[:, ::-1])
    img = np.zeros((H, W))
    cuts = (slice(0, -WIN), slice(-WIN, -SHIFT), slice(-SHIFT, None))
    for a, hs in enumerate(cuts):
        for b, ws in enumerate(cuts):
            img[hs, ws] = 3 * a + b
    m = img.reshape(STRIPS, WIN, WINS, WIN).transpose(0, 2, 3, 1).reshape(STRIPS, WINS, N)
    mask = np.where(m[:, :, None, :] != m[:, :, :, None], NEG, 0.0).astype(np.float32)
    both = mask[[0, STRIPS - 1]].transpose(2, 0, 1, 3)
    winmask = np.zeros((2, QROWS, 2, PAIRS, N), np.float32)
    for v in range(2):
        winmask[v, :N] = both[:, :, v::2]
    c["winmask"] = winmask.reshape(2 * QROWS, 2 * PAIRS * N)
    ch = np.arange(C)
    c["headmask"] = np.stack([(ch // D % 2 == hh) * np.float32(D ** -0.5) for hh in range(2)], 1).astype(np.float32)
    row = np.arange(PT) // N
    c["vmask"] = np.broadcast_to((row[:, None, None] == (np.arange(HEADS) % 2)[None, :, None]),
                                 (PT, HEADS, D)).astype(np.float32).reshape(PT, HEADS * D)
    i, o = np.arange(2 * MID)[:, None], np.arange(2 * MID)[None, :]
    c["groupmask"] = (i // 2 == o // 2).astype(np.float32)
    return c


class Strip:

    def __init__(self, k, c):
        self.k, self.c = k, c
        self.fixed = isinstance(k, int)
        self.n = c if self.fixed else 2 * k + c
        self.u = c % 2
        self.half = c // 2 if self.fixed else k + c // 2

    def back(self, d):
        return Strip(self.k, self.c - d)

    def there(self):
        return not self.fixed or 0 <= self.c < NS


def wait(e, sem, value):
    if not isinstance(value, int) or value > 0:
        e.wait_ge(sem, value)


def over_strips(e, body):
    for c in range(-1, 5):
        body(Strip(0, c))
    with e.Fori(0, (NS - 6) // 2) as k:
        body(Strip(k, 5))
        body(Strip(k, 6))
    for c in range(NS - 1, NS + 3):
        body(Strip(0, c))


def over_chunks(e, step, bias_steps):
    for c in range(CHUNKS + 2):
        step(0, c)
        bias_steps(c)
    with e.Fori(1, BPAIRS) as gp:
        for c in range(CHUNKS + 2):
            step(gp, c)


CONV_PREP = ["border", "half", "quarter", "relb_clear", "qt_clear", "st_clear",
             "bn_var", "bn_rstd", "bn_scale", "bn_shift", "bn_bias", "w2", "w2_hi", "w2_lo",
             "b3_var", "b3_rstd", "b3_scale", "b3_shift", "b3_bias", "w3"]
BIAS_PREP = ["abs", "exp", "ln", "positive", "softplus", "denominator", "sigmoid", "recip", "product", "magnitude",
             "sign", "scaled", "exponent", "power", "signed", "tab", "hidden_ps", "hidden", "table_ps", "table",
             "fc1_hi", "fc1_lo", "fc2_hi", "fc2_lo"]
PREP = CONV_PREP + BIAS_PREP


def program(nc, a, out):
    fp32 = mybir.dt.float32
    fp32r = mybir.dt.float32r
    ALU = mybir.AluOpType
    ACT = mybir.ActivationFunctionType
    AX = mybir.AxisListType
    ctx = ExitStack()
    with ctx:
        def sb(name, shape, dtype=fp32):
            return ctx.enter_context(nc.sbuf_tensor(name, shape, dtype))

        def sem(name):
            return ctx.enter_context(nc.semaphore(name))

        x1_dram = nc.dram_tensor("x1_scratch", (B, H + SHIFT, W, C), fp32, kind="Internal").ap()
        wrap_dram = nc.dram_tensor("wrap_scratch", (B, WIN, W, C), fp32, kind="Internal").ap()
        tb_dram = nc.dram_tensor("tb_scratch", (HEADS, REL), fp32, kind="Internal").ap()

        ident = sb("ident_sb", [128, 128])
        headmask = sb("headmask_sb", [C, 2])
        vmask = sb("vmask_sb", [PT, HEADS, D])
        winmask = sb("winmask_sb", [128, 2, PAIRS, N])
        groupmask = sb("groupmask_sb", [128, 2, MID])
        w1 = sb("w1_sb", [C, MID])
        w3 = sb("w3_sb", [128, C])
        bn = sb("bn", [128, 4, 2])
        bn_var, bn_rstd, bn_scale, bn_shift, bn_bias = [sb(f"bn_{i}", [128, 2]) for i in range(5)]
        b3 = sb("b3", [128, 4, C])
        b3_var, b3_rstd, b3_scale, b3_shift, b3_bias = [sb(f"b3_{i}", [128, C]) for i in range(5)]
        wqkv = sb("wqkv", [C, 3 * C])
        wproj = sb("wproj", [C, C])
        projb = sb("projb", [PT, C])
        ln = sb("ln", [C, 4])
        fc1b = sb("fc1b", [128, HC])
        fc2b = sb("fc2b", [PT, C])
        w2_parts, fc1_parts, fc2_parts = [[sb(f"{n}_{i}", shape, fp32r)[:] for i in ("hi", "lo")] for n, shape in (
            ("w2", [128, TAPS, 2 * MID]), ("fc1", [C, HID]), ("fc2", [128, HC, C]))]
        half = sb("half", [128, C])
        quarter = sb("quarter", [PT, 2, PAIRS])
        cpbw1 = sb("cpbw1", [2, CPB])
        cpbb1 = sb("cpbb1", [128, CPB // 128])
        cpbw2 = sb("cpbw2", [128, CPB // 128, HEADS])
        par = sb("par", [2, 4])
        par_abs, par_exp, par_ln, par_pos, par_sp = [sb(f"par_{i}", [2, 4]) for i in range(5)]
        sig_den, sig, ws2_recip = [sb(f"par1_{i}", [2, 1]) for i in range(3)]
        coords = sb("coords_sb", [2, REL])
        t_prod, t_mag, t_sign, t_scaled, t_exp, t_pow, t_signed, tab = [sb(f"tab{i}", [2, REL]) for i in range(8)]
        hid = sb("hid", [128, CPB // 128, REL])
        tb = sb("tb", [HEADS, REL])
        relb = sb("relb", [128, HEADS, N])
        biasm = sb("biasm", [128, 2, QUADS, PAIRS, 2, N])

        xc = sb("xc", [CT, CHUNKS, 2, TILES, C])
        xct = sb("xct", [C, 2, CHT])
        h1 = sb("h1", [128, 2, CHT])
        h1_parts = [sb(f"h1_{i}", [128, HP, HP], fp32r) for i in ("hi", "lo")]
        h2 = sb("h2", [128, 2, CHT])

        x1 = sb("x1", [PT, 2, PAIRS, C])
        xn = sb("xn", [PT, PAIRS, C])
        res1 = sb("res1", [PT, 2, PAIRS, C])
        res2 = sb("res2", [PT, 2, PAIRS, C])
        st = sb("st", [PT, 2, PAIRS, 6])
        lnp = sb("lnp", [PT, 10, 2, PAIRS])
        xt = sb("xt", [C, WINS, 2, N])
        qt = sb("qt", [C, WINS, QROWS])
        km = sb("km", [C, WINS, 2, N])
        vb = sb("vb", [PT, 2, WINS, HEADS, D])
        sc = sb("sc", [128, 2, QUADS, PAIRS, 2, N])
        mx = sb("mx", [128, 2, 2, PAIRS, 2])
        pt = sb("pt", [PT, PAIRS, QUADS, 2 * QROWS])
        staging = sc[:].rearrange("p u q k h m -> p (u q k h m)")
        w2raw, w2, fc1, fc2 = [staging[:, n0:n1] for n0, n1 in (
            (0, TAPS * MID), (TAPS * MID, 3 * TAPS * MID),
            (3 * TAPS * MID, 3 * TAPS * MID + HID), (3 * TAPS * MID + HID, 3 * TAPS * MID + 2 * HID))]
        w2raw = w2raw.rearrange("p (t o) -> p t o", t=TAPS)
        w2 = w2.rearrange("p (t o) -> p t o", t=TAPS)
        fc2 = fc2.rearrange("p (c o) -> p c o", c=HC)
        rsum, sums = [sb(i, [128, 2, 2, PAIRS, 2]) for i in ("rsum", "sums")]
        ot = sb("ot", [C, PAIRS, PT])
        x2 = sb("x2", [PT, PAIRS, C])
        z = sb("z", [PT, PAIRS, C])
        zt = sb("zt", [C, ST])
        zt_parts = [sb(f"zt_{i}", [C, ST], fp32r) for i in ("hi", "lo")]
        g = sb("g", [128, 2, ST])
        g_parts = [sb(f"g_{i}", [128, HC, ST], fp32r) for i in ("hi", "lo")]
        yt = sb("yt", [C, ST])
        y = sb("y", [PT, 2, PAIRS, C])

        bank = [ctx.enter_context(nc.psum_tensor(f"bank{i}", [128, 512], fp32)) for i in range(8)]
        RA, RB, RC = bank[4], bank[5:7], bank[7]
        A_JOBS = 3
        B_JOBS = 4
        SMALL = 6
        C_JOBS = 5

        conv_load, bias_load, wload, prep, tb_store, tb_load = sem("conv_load"), sem("bias_load"), sem("wload"), sem("prep"), sem("tb_store"), sem("tb_load")
        xc_in = [sem(f"xc_in{c}") for c in range(CHUNKS)]
        xc_out = [sem(f"xc_out{c}") for c in range(CHUNKS)]
        xct_ps = [sem(f"xct_ps{m}") for m in range(2)]
        xct_sb = [sem(f"xct_sb{m}") for m in range(2)]
        conv3_ps = [sem(f"conv3_ps{m}") for m in range(2)]
        xc_biased, xc_summed, xc_relu = sem("xc_biased"), sem("xc_summed"), sem("xc_relu")
        h1_split, zt_split, g_split = sem("h1_split"), sem("zt_split"), sem("g_split")
        conv1_ps, h1_sb, conv2_ps, h2_sb = sem("conv1_ps"), sem("h1_sb"), sem("conv2_ps"), sem("h2_sb")
        biasm_done = sem("biasm_done")
        x1_in = [sem(f"x1_in{u}") for u in range(2)]
        y_out = [sem(f"y_out{u}") for u in range(2)]
        wrapped = sem("wrapped")
        stats = [sem(f"stats_sem{i}") for i in range(2)]
        small = sem("small")
        xn_sb, z_sb, res1_sb, res2_sb = sem("xn_sb"), sem("z_sb"), sem("res1_sb"), sem("res2_sb")
        a_full, a_out, c_full, c_out = sem("a_full"), sem("a_out"), sem("c_full"), sem("c_out")
        hidden_full, hidden_out = sem("hidden_full"), sem("hidden_out")
        b_full = [sem(f"b_full{j}") for j in range(2)]
        b_out = [sem(f"b_out{j}") for j in range(2)]
        s_full, s_out, max_done, sub_done, exp_done = [sem(n) for n in
                                                       ("s_full", "s_out", "max_done", "sub_done", "exp_done")]
        sums_done, rsum_done, divided = sem("sums_done"), sem("rsum_done"), sem("divided")

        CONV_LOADS, BIAS_LOADS, LOADS = [], [], []

        def b_before(t, job):
            if job == 0:
                return B_JOBS * t.n - (B_JOBS - 1)
            return B_JOBS * t.n + job + (1 if t.back(-1).there() else 0)

        block_ = ctx.enter_context(nc.Block())

        def at(e, name):
            wait(e, prep, PREP.index(name))

        @block_.sync
        def _(sp):
            def conv_load_in(dst, src):
                CONV_LOADS.append(dst)
                sp.dma_start(dst, src).then_inc(conv_load, 16)

            def bias_load_in(dst, src):
                BIAS_LOADS.append(dst)
                sp.dma_start(dst, src).then_inc(bias_load, 16)

            def load(dst, src):
                LOADS.append(dst)
                sp.dma_start(dst, src).then_inc(wload, 16)

            def everywhere(name, parts, n=C):
                return bass.AP(tensor=a[name].tensor, offset=0, ap=[[0, parts], [1, n]])

            def column(name):
                return a[name].rearrange("(p o) -> p o", o=1)

            def chunk(dram, gp, c, m):
                return dram[2 * gp + m, ROWS * c:ROWS * c + ROWS].rearrange("(t r) w ch -> (r w) t ch", t=TILES)

            def chunk_in(gp, c):
                for m in range(2):
                    sp.dma_start(xc[:, c, m], chunk(a["x"], gp, c, m)).then_inc(xc_in[c], 16)

            def chunk_out(gp, c):
                sp.wait_ge(xc_relu, 2 * (CHUNKS * gp + c + 1))
                for m in range(2):
                    sp.dma_start(chunk(x1_dram, gp, c, m), xc[:, c, m]).then_inc(xc_out[c], 16)
                    if c == 0:
                        sp.dma_start(x1_dram[2 * gp + m, H:H + 2].rearrange("r w c -> (r w) c"),
                                     xc[:, 0, m, 0, :]).then_inc(xc_out[0], 16)
                        sp.dma_start(x1_dram[2 * gp + m, H + 2], xc[0:W, 0, m, 1, :]).then_inc(xc_out[0], 16)

            def twice(name):
                return bass.AP(tensor=a[name].tensor, offset=0, ap=[[0, 2], [1, MID], [1, 1]])

            for i, nm in enumerate("vgmb"):
                for l in range(2):
                    conv_load_in(bn[:, "gbmv".index(nm), l:l + 1], twice(f"{nm}{l + 1}"))
                conv_load_in(b3[:, "gbmv".index(nm), :], everywhere(f"{nm}3", 128))
            conv_load_in(w3[:], bass.AP(tensor=a["w3"].tensor, offset=0, ap=[[0, 2], [C, MID], [1, C]]))
            conv_load_in(groupmask[:], a["groupmask"].rearrange("p (m o) -> p m o", m=2))
            for t in range(TAPS):
                conv_load_in(w2raw[:, t, :], bass.AP(tensor=a["w2"].tensor, offset=t * 2 * MID,
                                                     ap=[[0, MID], [MID, 2], [1, MID]]))
            conv_load_in(w1[:], a["w1"])
            conv_load_in(ident[:], a["ident"])
            for c in range(CHUNKS):
                chunk_in(0, c)
            bias_load_in(coords[:], a["coords"])
            bias_load_in(cpbw1[:], a["cpb_w1T"])
            bias_load_in(cpbw2[:], a["cpb_w2T"].rearrange("(c p) n -> p c n", p=128))
            for i, nm in enumerate(("h_times", "ws_scalar", "ws_scalar2", "pow_para")):
                bias_load_in(par[:, i:i + 1], everywhere(nm, 2, 1))
            with nc.allow_non_contiguous_dma(reason="a few hundred elements, once"):
                bias_load_in(cpbb1[:], a["cpb_b1"].rearrange("(c p) -> p c", p=128))
            load(headmask[:], a["headmask"])
            load(vmask[:], a["vmask"].rearrange("p (h d) -> p h d", h=HEADS))
            load(winmask[:].rearrange("p a k m -> p (a k m)"), a["winmask"])
            load(wqkv[:], a["qkv_wT"])
            load(wproj[:], a["proj_wT"])
            load(fc1, a["fc1_wT"])
            load(fc2, a["fc2_wT"].rearrange("(c p) n -> p c n", p=128))
            with nc.allow_non_contiguous_dma(reason="a few hundred elements, once"):
                load(fc1b[:], a["fc1_b"].rearrange("(c p) -> p c", p=128))
            load(projb[:], everywhere("proj_b", PT))
            load(fc2b[:], everywhere("fc2_b", PT))
            for i, nm in enumerate(("norm1_w", "norm1_b", "norm2_w", "norm2_b")):
                load(ln[:, i:i + 1], column(nm))

            def spread_bias(nj):
                for v in range(2):
                    for ni in range(WIN):
                        first = REL - 1 - ((nj + WIN - 1) * (2 * WIN - 1) + ni + WIN - 1)
                        src = bass.AP(tensor=tb_dram.tensor, offset=first,
                                      ap=[[REL, HEADS], [2 * WIN - 1, WIN], [1, WIN]])
                        n = v * QROWS + nj * WIN + ni
                        sp.dma_start(relb[n:n + 1], src).then_inc(tb_load, 16)

            def chunks(gp, c):
                if c < CHUNKS:
                    chunk_out(gp, c)
                if c >= 2:
                    sp.wait_ge(xc_out[c - 2], (32 if c > 2 else 96) * (gp + 1))
                    chunk_in(gp + 1, c - 2)

            for c in range(CHUNKS + 2):
                chunks(0, c)
            sp.wait_ge(prep, PREP.index("table") + 1)
            sp.dma_start(tb_dram, tb[:]).then_inc(tb_store, 16)
            sp.wait_ge(tb_store, 16)
            for c in range(CHUNKS + 2):
                chunks(1, c)
                if c < WIN:
                    spread_bias(c)
            with sp.Fori(2, BPAIRS - 1) as gp:
                for c in range(CHUNKS + 2):
                    chunks(gp, c)
            def columns(p):
                c0 = 2 * WIN * p + SHIFT
                if p < PAIRS - 1:
                    return [(c0, 0, 2 * WIN)]
                return [(c0, 0, W - c0), (0, W - c0, 2 * WIN - (W - c0))]

            def block(dram, img, r, c, nj):
                d = dram[img, bass.ds(r, WIN), c:c + nj, :]
                return d.rearrange("i j c -> j i c")

            def load_strip(img, s, u):
                n = STRIPS * img + s
                wait(sp, xn_sb, n - 1)
                wait(sp, res1_sb, n - 1)
                for p in range(PAIRS):
                    for c, j0, nj in columns(p):
                        sp.dma_start(x1[WIN * j0:WIN * (j0 + nj), u, p, :],
                                     block(x1_dram, img, WIN * s + SHIFT, c, nj)).then_inc(x1_in[u], 16)

            def store_strip(img, s, u):
                sp.wait_ge(c_out, C_JOBS * (STRIPS * img + s + 1))
                wraps = s == STRIPS - 1
                dst, row = (wrap_dram, 0) if wraps else (out, WIN * s + SHIFT)
                for p in range(PAIRS):
                    for c, j0, nj in columns(p):
                        sp.dma_start(block(dst, img, row, c, nj),
                                     y[WIN * j0:WIN * (j0 + nj), u, p, :]).then_inc(y_out[u], 16)
                if wraps:
                    sp.wait_ge(y_out[u], 16 * MOVES * (STRIPS // 2) * (img + 1))
                    below = WIN - SHIFT
                    sp.dma_start(out[img, H - below:H], wrap_dram[img, 0:below]).then_inc(wrapped, 16)
                    sp.dma_start(out[img, 0:SHIFT], wrap_dram[img, below:WIN]).then_inc(wrapped, 16)

            for s in range(2):
                load_strip(0, s, s % 2)
            for c in range(CHUNKS):
                chunk_out(BPAIRS - 1, c)
            for c in range(CHUNKS):
                sp.wait_ge(xc_out[c], (32 if c else 96) * BPAIRS)
            for s in range(2, LEAD):
                load_strip(0, s, s % 2)
            with sp.Fori(0, B - 1) as img:
                for s in range(STRIPS):
                    if s + LEAD < STRIPS:
                        load_strip(img, s + LEAD, (s + LEAD) % 2)
                    else:
                        load_strip(img + 1, s + LEAD - STRIPS, (s + LEAD) % 2)
                    store_strip(img, s, s % 2)
            for s in range(STRIPS):
                if s + LEAD < STRIPS:
                    load_strip(B - 1, s + LEAD, (s + LEAD) % 2)
                store_strip(B - 1, s, s % 2)
            for u in range(2):
                sp.wait_ge(y_out[u], 16 * MOVES * (NS // 2))
            sp.wait_ge(wrapped, 32 * B)

        @block_.tensor
        def _(pe):
            def product(dst, left, right, start=True, stop=True):
                (l_hi, l_lo), (r_hi, r_lo) = left, right
                nc.tensor.matmul(dst, l_hi, r_hi, start=start, stop=False)
                nc.tensor.matmul(dst, l_hi, r_lo, start=False, stop=False)
                return nc.tensor.matmul(dst, l_lo, r_hi, start=False, stop=stop)

            def bias_steps(c):
                if c == 8:
                    at(pe, "hidden_ps")
                    for i in range(CPB // 128):
                        mm = nc.tensor.matmul(bank[6][:, REL * i:REL * i + REL], cpbw1[:, 128 * i:128 * i + 128],
                                              tab[:], start=True, stop=True)
                    mm.then_inc(prep, 1)
                    at(pe, "table_ps")
                    for i in range(CPB // 128):
                        mm = nc.tensor.matmul(bank[7][0:HEADS, 0:REL], cpbw2[:, i, :], hid[:, i, :],
                                              start=i == 0, stop=i == CPB // 128 - 1)
                    mm.then_inc(prep, 1)

            pe.wait_ge(conv_load, 16 * len(CONV_LOADS))

            def x_to_channels(gp, c):
                n = CHUNKS * gp + c
                pe.wait_ge(xc_in[c], 32 * (gp + 1))
                for m in range(2):
                    wait(pe, xct_sb[m], n)
                    for t in range(TILES):
                        mm = nc.tensor.transpose(bank[m][:, CT * t:CT * t + CT], xc[:, c, m, t, :],
                                                 ident[0:CT, 0:CT])
                    mm.then_inc(xct_ps[m], 1)

            def conv1(gp, c):
                n = CHUNKS * gp + c
                wait(pe, h1_sb, n)
                for m in range(2):
                    pe.wait_ge(xct_sb[m], n + 1)
                    mm = nc.tensor.matmul(bank[2][MID * m:MID * m + MID, 0:CHT], w1[:], xct[:, m, :],
                                          start=True, stop=True)
                mm.then_inc(conv1_ps, 1)

            def conv2(gp, c):
                n = CHUNKS * gp + c
                if isinstance(gp, int) and c == 0:
                    at(pe, "b3_var")
                pe.wait_ge(h1_split, n + (2 if c < CHUNKS - 1 else 1))
                wait(pe, h2_sb, n)
                for t in range(TAPS):
                    dy, dx = divmod(t, 3)
                    mm = product(bank[3][:, 0:CHT], [w[:, t] for w in w2_parts],
                                 [h[:, ROWS * c + dy:ROWS * c + dy + ROWS, dx:dx + W] for h in h1_parts],
                                 t == 0, t == TAPS - 1)
                mm.then_inc(conv2_ps, 1)

            def conv3(gp, c):
                n = CHUNKS * gp + c
                if isinstance(gp, int) and c == 0:
                    pe.wait_ge(prep, len(CONV_PREP))
                pe.wait_ge(h2_sb, n + 1)
                wait(pe, xc_summed, 2 * n)
                for m in range(2):
                    for t in range(TILES):
                        mm = nc.tensor.matmul(bank[4 + m][0:CT, C * t:C * t + C],
                                              h2[MID * m:MID * m + MID, c % 2, CT * t:CT * t + CT],
                                              w3[MID * m:MID * m + MID, :], start=True, stop=True)
                    mm.then_inc(conv3_ps[m], 1)

            def convs(gp, c):
                if c == 0:
                    x_to_channels(gp, 0)
                if c < CHUNKS:
                    conv1(gp, c)
                if c + 1 < CHUNKS:
                    x_to_channels(gp, c + 1)
                if c >= 2:
                    conv3(gp, c - 2)
                if 1 <= c <= CHUNKS:
                    conv2(gp, c - 1)

            over_chunks(pe, convs, bias_steps)
            pe.wait_ge(prep, len(PREP))
            pe.wait_ge(h2_sb, CHUNKS * BPAIRS)
            pe.wait_ge(xc_summed, 2 * CHUNKS * BPAIRS)

            def to_channels(ring, src, full):
                for p in range(PAIRS):
                    mm = nc.tensor.transpose(ring[:, PT * p:PT * p + PT], src[:, p, :], ident[0:PT, 0:PT])
                mm.then_inc(full, 1)

            def values(t, j):
                wait(pe, b_out[j], b_before(t, 0))
                for w in range(4):
                    rows = xt[:, 4 * j + w].rearrange("c v n -> c (v n)")
                    mm = nc.tensor.matmul(RB[j][0:PT, C * w:C * w + C], rows, wqkv[:, 2 * C:3 * C],
                                          start=True, stop=True)
                mm.then_inc(b_full[j], 1)

            def project(t, i):
                wait(pe, a_out, A_JOBS * t.n + 1 + i)
                nc.tensor.matmul(RA[:, 0:ST], wqkv[:, C * i:C * i + C], xt[:, :, 0, :],
                                 start=True, stop=True).then_inc(a_full, 1)

            def scores(t, r, i):
                pe.wait_ge(a_out, A_JOBS * t.n + 3)
                wait(pe, s_out, QUADS * (t.n - 1) + 2 * r + 2)
                for w in range(4 * i, 4 * i + 4):
                    p, v = divmod(w, 2)
                    for q in (2 * r, 2 * r + 1):
                        mm = nc.tensor.matmul(bank[q][QROWS * v:QROWS * v + QROWS, 2 * N * p:2 * N * p + 2 * N],
                                              qt[32 * q:32 * q + 32, w],
                                              km[32 * q:32 * q + 32, w].rearrange("p h m -> p (h m)"),
                                              start=True, stop=True)
                if i == 1:
                    mm.then_inc(s_full, 1)

            def probs_t(t, j):
                if j == 0:
                    pe.wait_ge(divided, 2 * t.n + 2)
                wait(pe, b_out[j % 2], b_before(t, 1 + j // 2))
                for q in range(QUADS):
                    mm = nc.tensor.transpose(RB[j % 2][0:PT, 128 * q:128 * q + 128],
                                             sc[:, t.u, q, j].rearrange("p h m -> p (h m)"), ident[:])
                mm.then_inc(b_full[j % 2], 1)

            def attend(t, j):
                wait(pe, b_out[0], b_before(t, 3))
                wait(pe, b_out[1], b_before(t, 2 + j))
                for w in range(4 * j, 4 * j + 4):
                    p, v = divmod(w, 2)
                    for q in range(QUADS):
                        mm = nc.tensor.matmul(RB[0][32 * q:32 * q + 32, N * w:N * w + N],
                                              vb[:, t.u, w, 2 * q:2 * q + 2].rearrange("p h d -> p (h d)"),
                                              pt[:, p, q, QROWS * v:QROWS * v + N], start=True, stop=True)
                if j == 1:
                    mm.then_inc(b_full[0], 1)

            def projection(t):
                wait(pe, b_out[0], b_before(t, 4))
                for p in range(PAIRS):
                    mm = nc.tensor.matmul(RB[1][0:PT, C * p:C * p + C], ot[:, p, :], wproj[:],
                                          start=True, stop=True)
                mm.then_inc(b_full[1], 1)

            def hidden(t, j):
                pe.wait_ge(zt_split, t.n + 1)
                if j % 2 == 0:
                    ring, full = RC, c_full
                    wait(pe, c_out, C_JOBS * t.n + 1 + j // 2)
                else:
                    ring, full = RA, hidden_full
                    ahead = min(t.n + 4, NS) if t.fixed else t.n + 4
                    wait(pe, a_out, A_JOBS * ahead)
                    wait(pe, hidden_out, 2 * t.n + j // 2)
                product(ring[:, 0:ST], [w[:, 128 * j:128 * j + 128] for w in fc1_parts],
                        [z[:] for z in zt_parts]).then_inc(full, 1)

            def mlp_out(t, r):
                pe.wait_ge(g_split, HC * t.n + 2 * r + 2)
                wait(pe, c_out, C_JOBS * t.n + 3)
                for c in (2 * r, 2 * r + 1):
                    mm = product(RC[:, 0:ST], [w[:, c, :] for w in fc2_parts], [g_[:, c, :] for g_ in g_parts],
                                 c == 0, c == HC - 1)
                if r == 1:
                    mm.then_inc(c_full, 1)

            def mlp_to_tokens(t):
                pe.wait_ge(c_out, C_JOBS * t.n + 4)
                for p in range(PAIRS):
                    mm = nc.tensor.transpose(RC[0:PT, C * p:C * p + C], yt[:, PT * p:PT * p + PT], ident[:])
                mm.then_inc(c_full, 1)

            def strips(t):
                ahead, t1, t2, t3 = t.back(-1), t.back(1), t.back(2), t.back(3)
                if t.there():
                    pe.wait_ge(a_out, A_JOBS * t.n + 1)
                    project(t, 0)
                if t3.there():
                    pe.wait_ge(z_sb, t3.n + 1)
                    wait(pe, c_out, C_JOBS * t3.n)
                    to_channels(RC, z, c_full)
                if t.there():
                    values(t, 0)
                    project(t, 1)
                    values(t, 1)
                if t3.there():
                    hidden(t3, 0)
                if t.there():
                    scores(t, 0, 0)
                    scores(t, 0, 1)
                if t3.there():
                    hidden(t3, 1)
                if t.there():
                    scores(t, 1, 0)
                if t3.there():
                    hidden(t3, 2)
                if t.there():
                    scores(t, 1, 1)
                if t1.there():
                    probs_t(t1, 0)
                    probs_t(t1, 1)
                if t3.there():
                    hidden(t3, 3)
                if t1.there():
                    probs_t(t1, 2)
                    probs_t(t1, 3)
                if t3.there():
                    mlp_out(t3, 0)
                if t1.there():
                    attend(t1, 0)
                if t3.there():
                    mlp_out(t3, 1)
                if t1.there():
                    attend(t1, 1)
                if ahead.there():
                    pe.wait_ge(xn_sb, ahead.n + 1)
                    wait(pe, a_out, A_JOBS * ahead.n)
                    if t3.there():
                        pe.wait_ge(hidden_out, 2 * t3.n + 2)
                    to_channels(RA, xn, a_full)
                if t3.there():
                    mlp_to_tokens(t3)
                if t1.there():
                    projection(t1)

            over_strips(pe, strips)

        @block_.scalar
        def _(act):
            def step(name, *args, **kw):
                at(act, name)
                nc.scalar.activation(*args, **kw).then_inc(prep, 1)

            def bias_steps(c):
                if c == 1:
                    act.wait_ge(bias_load, 16 * len(BIAS_LOADS))
                    step("abs", par_abs[:, 0:3], par[:, 0:3], ACT.Abs)
                    at(act, "exp")
                    nc.scalar.activation(par_exp[:, 3:4], par[:, 3:4], ACT.Exp, scale=-1.0)
                    nc.scalar.activation(par_exp[:, 0:3], par_abs[:, 0:3], ACT.Exp, scale=-1.0).then_inc(prep, 1)
                    step("ln", par_ln[:, 0:3], par_exp[:, 0:3], ACT.Ln, bias=1.0)
                if c == 3:
                    step("magnitude", t_mag[:], t_prod[:], ACT.Abs)
                    step("sign", t_sign[:], t_prod[:], ACT.Sign)
                if c == 8:
                    at(act, "hidden")
                    for i in range(CPB // 128):
                        ins = nc.scalar.activation(hid[:, i, :], bank[6][:, REL * i:REL * i + REL], ACT.Relu,
                                                   bias=cpbb1[:, i:i + 1])
                    ins.then_inc(prep, 1)
                    step("table", tb[:], bank[7][0:HEADS, 0:REL], ACT.Copy)


            def xct_out(gp, c):
                n = CHUNKS * gp + c
                act.wait_ge(xct_ps[0], n + 1)
                wait(act, conv1_ps, n)
                nc.scalar.activation(xct[:, 0, :], bank[0][:, 0:CHT], ACT.Copy).then_inc(xct_sb[0], 1)

            def h1_out(gp, c):
                n = CHUNKS * gp + c
                if isinstance(gp, int) and c == 0:
                    at(act, "w2")
                act.wait_ge(conv1_ps, n + 1)
                wait(act, h1_split, n - 1 if c else n)
                ps, norm = bank[2][:, 0:CHT], {"scale": bn_scale[:, 0:1], "bias": bn_bias[:, 0:1]}
                nc.scalar.activation(h1_parts[0][:, 1 + ROWS * c:1 + ROWS * c + ROWS, 1:1 + W],
                                     ps.rearrange("p (r w) -> p r w", w=W), ACT.Relu, **norm)
                nc.scalar.activation(h1[:, c % 2], ps, ACT.Relu, **norm).then_inc(h1_sb, 1)

            def h2_out(gp, c):
                n = CHUNKS * gp + c
                act.wait_ge(conv2_ps, n + 1)
                wait(act, conv3_ps[1], n if c == 0 else CHUNKS * gp + max(c - 1, 0))
                nc.scalar.activation(h2[:, c % 2, :], bank[3][:, 0:CHT], ACT.Relu,
                                     scale=bn_scale[:, 1:2], bias=bn_bias[:, 1:2]).then_inc(h2_sb, 1)

            def relu_out(gp, c):
                n = CHUNKS * gp + c
                for m in range(2):
                    act.wait_ge(xc_summed, 2 * n + m + 1)
                    nc.scalar.activation(xc[:, c, m], xc[:, c, m], ACT.Relu).then_inc(xc_relu, 1)

            def convs(gp, c):
                if c == 0:
                    xct_out(gp, 0)
                if c < CHUNKS:
                    h1_out(gp, c)
                if c + 1 < CHUNKS:
                    xct_out(gp, c + 1)
                if c >= 2:
                    relu_out(gp, c - 2)
                if 1 <= c <= CHUNKS:
                    h2_out(gp, c - 1)

            over_chunks(act, convs, bias_steps)

            def xt_out(t):
                act.wait_ge(a_full, A_JOBS * t.n + 1)
                for v in range(2):
                    i = nc.scalar.activation(xt[:, :, v, :], RA[:, 0:ST].rearrange("c (w n) -> c w n", n=N),
                                             ACT.Identity, scale=ln[:, 0:1], bias=ln[:, 1:2])
                i.then_inc(a_out, 1)

            def q_out(t):
                act.wait_ge(a_full, A_JOBS * t.n + 2)
                wait(act, s_full, 2 * t.n)
                nc.scalar.activation(qt[:, :, 0:N], RA[:, 0:ST].rearrange("c (w n) -> c w n", n=N),
                                     ACT.Copy).then_inc(a_out, 1)

            def k_out(t):
                act.wait_ge(a_full, A_JOBS * t.n + 3)
                for hh in range(2):
                    i = nc.scalar.activation(km[:, :, hh, :], RA[:, 0:ST].rearrange("c (w n) -> c w n", n=N),
                                             ACT.Identity, scale=headmask[:, hh:hh + 1])
                i.then_inc(a_out, 1)

            def zt_out(t):
                act.wait_ge(c_full, C_JOBS * t.n + 1)
                for dst in (zt_parts[0], zt):
                    i = nc.scalar.activation(dst[:], RC[:, 0:ST], ACT.Identity, scale=ln[:, 2:3], bias=ln[:, 3:4])
                i.then_inc(c_out, 1)

            def gelu(t, j):
                ring, full, out_, n = ((RC, c_full, c_out, C_JOBS * t.n + 2 + j // 2) if j % 2 == 0 else
                                       (RA, hidden_full, hidden_out, 2 * t.n + 1 + j // 2))
                act.wait_ge(full, n)
                wait(act, g_split, HC * t.n + j - 1)
                for dst in (g_parts[0][:, j], g[:, j % 2]):
                    i = nc.scalar.activation(dst, ring[:, 0:ST], ACT.Gelu, bias=fc1b[:, j:j + 1])
                i.then_inc(out_, 1)

            def yt_out(t):
                act.wait_ge(c_full, C_JOBS * t.n + 4)
                nc.scalar.activation(yt[:], RC[:, 0:ST], ACT.Copy).then_inc(c_out, 1)

            def pt_out(t, j):
                act.wait_ge(b_full[j % 2], b_before(t, 1 + j // 2) + 1)
                nc.scalar.activation(pt[:, j].rearrange("p q n -> p (q n)"), RB[j % 2][0:PT, :],
                                     ACT.Copy).then_inc(b_out[j % 2], 1)

            def ot_out(t):
                act.wait_ge(b_full[0], b_before(t, 3) + 1)
                nc.scalar.activation(ot[:].rearrange("c p n -> c (p n)"), RB[0][:, 0:ST],
                                     ACT.Copy).then_inc(b_out[0], 1)

            def exponentials(t, r):
                act.wait_ge(sub_done, 2 * t.n + r + 1)
                half_sc = sc[:, t.u, 2 * r:2 * r + 2].rearrange("p q k h m -> p (q k h m)")
                nc.scalar.activation(half_sc, half_sc, ACT.Exp).then_inc(exp_done, 1)

            def strips(t):
                ahead, t1, t2, t3 = t.back(-1), t.back(1), t.back(2), t.back(3)
                if t.there():
                    q_out(t)
                if t3.there():
                    zt_out(t3)
                if t.there():
                    k_out(t)
                if t3.there():
                    gelu(t3, 0)
                    gelu(t3, 1)
                    gelu(t3, 2)
                if t1.there():
                    pt_out(t1, 0)
                    pt_out(t1, 1)
                if t3.there():
                    gelu(t3, 3)
                if t1.there():
                    pt_out(t1, 2)
                    pt_out(t1, 3)
                if t.there():
                    exponentials(t, 0)
                if t3.there():
                    yt_out(t3)
                if t1.there():
                    ot_out(t1)
                if ahead.there():
                    xt_out(ahead)
                if t.there():
                    exponentials(t, 1)

            over_strips(act, strips)

        def norm_stats(i, t, src):
            for p in range(PAIRS):
                ins = nc.vector.bn_stats(st[:, i, p, :], src[:, p, :])
            ins.then_inc(stats[i], 1)

        @block_.vector
        def _(dve):
            def step(name, f, *args, **kw):
                at(dve, name)
                f(*args, **kw).then_inc(prep, 1)

            V = nc.vector

            def rest(trailing, x, leading):
                return V.tensor_tensor(out=trailing, in0=x, in1=leading.bitcast(fp32), op=ALU.subtract)

            def split_weights(name, w, parts):
                step(f"{name}_hi", V.tensor_copy, parts[0], w)
                at(dve, f"{name}_lo")
                rest(parts[1], w, parts[0]).then_inc(prep, 1)

            at(dve, "border")
            for h in h1_parts:
                i = V.memset(h[:].bitcast(fp32), 0.0)
            i.then_inc(prep, 1)
            at(dve, "w2")
            for t in range(TAPS):
                i = V.tensor_tensor(out=w2[:, t].rearrange("p (m o) -> p m o", m=2), in0=w2raw[:, t].unsqueeze(1).to_broadcast([128, 2, MID]),
                                    in1=groupmask[:], op=ALU.mult)
            i.then_inc(prep, 1)
            split_weights("w2", w2, w2_parts)

            def bias_steps(c):
                if c == 2:
                    step("positive", V.tensor_scalar, par_pos[:, 0:3], par[:, 0:3], 0.0, None, ALU.max)
                    step("softplus", V.tensor_tensor, out=par_sp[:, 0:3], in0=par_pos[:, 0:3], in1=par_ln[:, 0:3],
                         op=ALU.add)
                    step("denominator", V.tensor_scalar, sig_den[:], par_exp[:, 3:4], 1.0, None, ALU.add)
                    step("sigmoid", V.reciprocal, sig[:], sig_den[:])
                    step("recip", V.reciprocal, ws2_recip[:], par_sp[:, 2:3])
                    step("product", V.tensor_scalar, t_prod[:], coords[:], par_sp[:, 0:1], None, ALU.mult)
                if c == 4:
                    step("scaled", V.tensor_scalar, t_scaled[:], t_mag[:], par_sp[:, 1:2], 1e-6, ALU.mult, ALU.add)
                    step("exponent", V.tensor_copy, t_exp[:], sig[:].to_broadcast([2, REL]))
                if c == 7:
                    step("signed", V.tensor_tensor, out=t_signed[:], in0=t_sign[:], in1=t_pow[:], op=ALU.mult)
                    step("tab", V.tensor_scalar, tab[:], t_signed[:], ws2_recip[:], None, ALU.mult)
                if c == 8:
                    dve.wait_ge(wload, 16 * len(LOADS))
                    split_weights("fc1", fc1, fc1_parts)
                    split_weights("fc2", fc2, fc2_parts)


            def xct_out(gp, c):
                n = CHUNKS * gp + c
                dve.wait_ge(xct_ps[1], n + 1)
                wait(dve, conv1_ps, n)
                V.tensor_copy(xct[:, 1, :], bank[1][:, 0:CHT]).then_inc(xct_sb[1], 1)

            def h1_rest(gp, c):
                dve.wait_ge(h1_sb, CHUNKS * gp + c + 1)
                hi, lo = [h[:, 1 + ROWS * c:1 + ROWS * c + ROWS, 1:1 + W] for h in h1_parts]
                rest(lo, h1[:, c % 2].rearrange("p (r w) -> p r w", w=W), hi).then_inc(h1_split, 1)

            def sum_out(gp, c):
                n = CHUNKS * gp + c
                dve.wait_ge(xc_biased, n + 1)
                for m in range(2):
                    dve.wait_ge(conv3_ps[m], n + 1)
                    x_m = xc[:, c, m].rearrange("p t c -> p (t c)")
                    V.tensor_tensor(out=x_m, in0=bank[4 + m][0:CT, :], in1=x_m, op=ALU.add).then_inc(xc_summed, 1)

            def convs(gp, c):
                if c == 0:
                    xct_out(gp, 0)
                if c + 1 < CHUNKS:
                    xct_out(gp, c + 1)
                if c < CHUNKS:
                    h1_rest(gp, c)
                if c >= 2:
                    sum_out(gp, c - 2)

            over_chunks(dve, convs, bias_steps)

            def bias_and_mask():
                dve.wait_ge(tb_load, 16 * 2 * N)
                for kind in range(2):
                    for h in range(HEADS):
                        i = V.tensor_tensor(out=biasm[:, kind, h // 2, :, h % 2, :], in0=winmask[:, kind],
                                            in1=relb[:, h].unsqueeze(1).to_broadcast([128, PAIRS, N]), op=ALU.add)
                i.then_inc(biasm_done, 1)
                dve.wait_ge(biasm_done, 1)

            def v_out(t, j):
                dve.wait_ge(b_full[j], b_before(t, 0) + 1 if t.c or not t.fixed else 1)
                V.tensor_tensor(out=vb[:, t.u, 4 * j:4 * j + 4],
                                in0=RB[j][0:PT, :].rearrange("p (w h d) -> p w h d", w=4, h=HEADS),
                                in1=vmask[:].unsqueeze(1).to_broadcast([PT, 4, HEADS, D]),
                                op=ALU.mult).then_inc(b_out[j], 1)

            def zt_rest(t):
                dve.wait_ge(c_out, C_JOBS * t.n + 1)
                rest(zt_parts[1][:], zt[:], zt_parts[0][:]).then_inc(zt_split, 1)

            def g_rest(t, j):
                if j % 2 == 0:
                    dve.wait_ge(c_out, C_JOBS * t.n + 2 + j // 2)
                else:
                    dve.wait_ge(hidden_out, 2 * t.n + 1 + j // 2)
                rest(g_parts[1][:, j], g[:, j % 2], g_parts[0][:, j]).then_inc(g_split, 1)

            def biased(t, r):
                dve.wait_ge(s_full, 2 * t.n + r + 1)
                for q in (2 * r, 2 * r + 1):
                    if t.u == 0:
                        b = biasm[:, 0, q]
                    elif t.fixed:
                        b = biasm[:, int(t.n % STRIPS == STRIPS - 1), q]
                    else:
                        b = biasm[:, bass.ds((t.half % (STRIPS // 2)) // (STRIPS // 2 - 1), 1), q]
                        b = b.rearrange("p o k h m -> p (o k) h m")
                    V.tensor_tensor(out=sc[:, t.u, q].rearrange("p k h m -> p (k h m)"), in0=bank[q][:, 0:ST],
                                    in1=b.rearrange("p k h m -> p (k h m)"), op=ALU.add).then_inc(s_out, 1)

            def maxima(t, r):
                wait(dve, sub_done, 2 * (t.n - 1) + r + 1)
                dve.wait_ge(s_out, QUADS * t.n + 2 * r + 2)
                V.reduce_max(mx[:, r].rearrange("p q k h -> p (q k h)"),
                             sc[:, t.u, 2 * r:2 * r + 2].rearrange("p q k h m -> p (q k h) m"),
                             AX.X).then_inc(max_done, 1)

            def row_sums(t, r):
                dve.wait_ge(exp_done, 2 * t.n + r + 1)
                wait(dve, divided, 2 * (t.n - 1) + r + 1)
                V.reduce_sum(sums[:, r].rearrange("p q k h -> p (q k h)"),
                             sc[:, t.u, 2 * r:2 * r + 2].rearrange("p q k h m -> p (q k h) m"),
                             AX.X).then_inc(sums_done, 1)
                dve.wait_ge(sums_done, 2 * t.n + r + 1)
                V.reciprocal(rsum[:, r].rearrange("p q k h -> p (q k h)"),
                             sums[:, r].rearrange("p q k h -> p (q k h)")).then_inc(rsum_done, 1)

            def x1_stats(t):
                dve.wait_ge(x1_in[t.u], 16 * MOVES * (t.half + 1))
                wait(dve, small, SMALL * t.n)
                norm_stats(0, t, x1[:, t.u])

            def norm(i, round_, src, dst, done):
                dve.wait_ge(small, SMALL * round_ + SMALL)
                for p in range(PAIRS):
                    ins = V.tensor_scalar(dst[:, p, :], src[:, p, :], lnp[:, 8, i, p:p + 1], lnp[:, 9, i, p:p + 1],
                                          ALU.mult, ALU.add)
                ins.then_inc(done, 1)

            def x1_norm(t):
                wait(dve, a_full, A_JOBS * (t.n - 1) + 1)
                norm(0, t.n, x1[:, t.u], xn, xn_sb)

            def x2_norm(t):
                wait(dve, c_full, C_JOBS * (t.n - 1) + 1)
                norm(1, t.n + 3, x2, z, z_sb)

            def x2_out(t):
                dve.wait_ge(b_full[1], b_before(t, 3) + 1)
                dve.wait_ge(res1_sb, t.n + 1)
                wait(dve, res2_sb, t.n)
                wait(dve, z_sb, t.n)
                V.tensor_tensor(out=x2[:].rearrange("p k c -> p (k c)"), in0=RB[1][0:PT, :],
                                in1=res1[:, t.u].rearrange("p k c -> p (k c)"), op=ALU.add).then_inc(b_out[1], 1)
                dve.wait_ge(b_out[1], b_before(t, 4))
                dve.wait_ge(small, SMALL * (t.n + 3))
                norm_stats(1, t, x2)

            def y_sum(t):
                dve.wait_ge(c_full, C_JOBS * t.n + 5)
                wait(dve, y_out[t.u], 16 * MOVES * t.half)
                dve.wait_ge(res2_sb, t.n + 1)
                V.tensor_tensor(out=y[:, t.u].rearrange("p k c -> p (k c)"), in0=RC[0:PT, :],
                                in1=res2[:, t.u].rearrange("p k c -> p (k c)"), op=ALU.add).then_inc(c_out, 1)

            def strips(t):
                ahead, t1, t2, t3 = t.back(-1), t.back(1), t.back(2), t.back(3)
                if t.there():
                    v_out(t, 0)
                if t3.there():
                    zt_rest(t3)
                if t.there():
                    v_out(t, 1)
                if t1.there():
                    row_sums(t1, 1)
                if ahead.there():
                    x1_stats(ahead)
                if t.fixed and t.c == 0:
                    bias_and_mask()
                if t.there():
                    biased(t, 0)
                if t3.there():
                    g_rest(t3, 0)
                if t.there():
                    maxima(t, 0)
                if t3.there():
                    g_rest(t3, 1)
                if t.there():
                    biased(t, 1)
                if t3.there():
                    g_rest(t3, 2)
                if t.there():
                    maxima(t, 1)
                if t3.there():
                    g_rest(t3, 3)
                if ahead.there():
                    x1_norm(ahead)
                if t2.there():
                    x2_norm(t2)
                if t.there():
                    row_sums(t, 0)
                if t3.there():
                    y_sum(t3)
                if t1.there():
                    x2_out(t1)

            over_strips(dve, strips)

        @block_.gpsimd
        def _(pool):
            P = nc.gpsimd

            def step(name, f, *args, **kw):
                at(pool, name)
                f(*args, **kw).then_inc(prep, 1)

            def tt(o, x, y_, op):
                return P.tensor_tensor(out=o, in0=x, in1=y_, op=op)

            step("half", P.memset, half[:], -0.5)
            step("quarter", P.memset, quarter[:], 0.25)
            step("relb_clear", P.memset, relb[:], 0.0)
            step("qt_clear", P.memset, qt[:], 0.0)
            step("st_clear", P.memset, st[:], 0.0)
            pool.wait_ge(conv_load, 16 * len(CONV_LOADS))
            for n, v, shift_, rstd_, scale_, bias_, q in (
                    ("bn", bn, bn_shift, bn_rstd, bn_scale, bn_bias, bn_var),
                    ("b3", b3, b3_shift, b3_rstd, b3_scale, b3_bias, b3_var)):
                step(f"{n}_var", P.tensor_scalar, q[:], v[:, 3], BN_EPS, None, ALU.add)
                step(f"{n}_rstd", tt, rstd_[:], q[:], half[:, 0:q.shape[1]], ALU.pow)
                step(f"{n}_scale", tt, scale_[:], v[:, 0], rstd_[:], ALU.mult)
                step(f"{n}_shift", tt, shift_[:], v[:, 2], scale_[:], ALU.mult)
                step(f"{n}_bias", tt, bias_[:], v[:, 1], shift_[:], ALU.subtract)
            step("w3", tt, w3[:], w3[:], b3_scale[:], ALU.mult)

            def convs(gp, c):
                if c < CHUNKS:
                    n = CHUNKS * gp + c
                    pool.wait_ge(xct_ps[1], n + 1)
                    x_c = xc[:, c].rearrange("p m t c -> p (m t) c")
                    P.tensor_tensor(out=x_c, in0=x_c, in1=b3_bias[0:CT].unsqueeze(1).to_broadcast(
                        [CT, 2 * TILES, C]), op=ALU.add).then_inc(xc_biased, 1)

            def bias_steps(c):
                if c == 4:
                    step("power", tt, t_pow[:], t_scaled[:], t_exp[:], ALU.pow)

            pool.wait_ge(prep, len(CONV_PREP))
            over_chunks(pool, convs, bias_steps)
            pool.wait_ge(prep, len(PREP))

            def factors(t):
                ahead, t2, before = t.back(-1), t.back(2), SMALL * (t.n + 1)
                _, mean_e, dev_e, _, mean_o, dev_o = [st[:, :, :, k] for k in range(6)]
                sum_, dif, dev, dif2, dev_eps, dif4, var, negm, rstd, shift = [lnp[:, k] for k in range(10)]
                half_ = half[0:PT, 0:2 * PAIRS].rearrange("p (i k) -> p i k", i=2)
                if ahead.there():
                    pool.wait_ge(stats[0], ahead.n + 1)
                if t2.there():
                    pool.wait_ge(stats[1], t2.n + 1)
                tt(sum_, mean_e, mean_o, ALU.add)
                tt(dif, mean_e, mean_o, ALU.subtract)
                tt(dev, dev_e, dev_o, ALU.add).then_inc(small, 1)
                pool.wait_ge(small, before + 1)
                tt(dif2, dif, dif, ALU.mult)
                P.tensor_scalar(dev_eps, dev, 1.0 / C, LN_EPS, ALU.mult, ALU.add)
                tt(negm, sum_, half_, ALU.mult).then_inc(small, 1)
                pool.wait_ge(small, before + 2)
                tt(dif4, dif2, quarter[:], ALU.mult).then_inc(small, 1)
                pool.wait_ge(small, before + 3)
                tt(var, dif4, dev_eps, ALU.add).then_inc(small, 1)
                pool.wait_ge(small, before + 4)
                wait(pool, xn_sb, min(ahead.n, NS) if ahead.fixed else ahead.n)
                wait(pool, z_sb, t2.n)
                tt(rstd, var, half_, ALU.pow).then_inc(small, 1)
                pool.wait_ge(small, before + 5)
                tt(shift, negm, rstd, ALU.mult).then_inc(small, 1)

            def add_bias(res, src, bias, done):
                P.tensor_tensor(out=res, in0=src, in1=bias[:].unsqueeze(1).to_broadcast([PT, PAIRS, C]),
                                op=ALU.add).then_inc(done, 1)

            def residual1(t):
                pool.wait_ge(stats[0], t.n + 1)
                wait(pool, b_out[1], b_before(t.back(2), 4) if t.back(2).there() else 0)
                add_bias(res1[:, t.u], x1[:, t.u], projb, res1_sb)

            def residual2(t):
                pool.wait_ge(b_out[1], b_before(t, 4))
                wait(pool, c_out, C_JOBS * (t.n - 1))
                add_bias(res2[:, t.u], x2[:], fc2b, res2_sb)

            def subtract(t):
                for r in range(2):
                    pool.wait_ge(max_done, 2 * t.n + r + 1)
                    s_r = sc[:, t.u, 2 * r:2 * r + 2].rearrange("p q k h m -> p (q k h) m")
                    m_r = mx[:, r].rearrange("p q k h -> p (q k h)").unsqueeze(2)
                    P.tensor_tensor(out=s_r, in0=s_r, in1=m_r.to_broadcast([128, 2 * HEADS, N]),
                                    op=ALU.subtract).then_inc(sub_done, 1)

            def divide(t):
                for r in range(2):
                    pool.wait_ge(rsum_done, 2 * t.n + r + 1)
                    p_r = sc[:, t.u, 2 * r:2 * r + 2].rearrange("p q k h m -> p (q k h) m")
                    r_r = rsum[:, r].rearrange("p q k h -> p (q k h)").unsqueeze(2)
                    P.tensor_tensor(out=p_r, in0=p_r, in1=r_r.to_broadcast([128, 2 * HEADS, N]),
                                    op=ALU.mult).then_inc(divided, 1)

            def strips(t):
                ahead, t1, t2 = t.back(-1), t.back(1), t.back(2)
                if t1.there():
                    divide(t1)
                if ahead.there() or t2.there():
                    factors(t)
                if t.there():
                    subtract(t)
                if t2.there():
                    residual2(t2)
                if ahead.there():
                    residual1(ahead)

            over_strips(pool, strips)


_OUT = (B, H, W, C)


def kernel(**inputs):
    import concourse.bacc as bacc
    from concourse.bass_utils import run_bass_kernel_spmd as run

    def arr(name):
        return np.ascontiguousarray(inputs[name])

    arrays = {"x": arr("x")}
    for i in "123":
        for v in "gbmv":
            arrays[v + i] = arr(f"L0_conv_{v}{i}")
    arrays["w1"] = arr("L0_conv_w1").reshape(C, MID)
    arrays["w2"] = arr("L0_conv_w2").reshape(-1)
    arrays["w3"] = arr("L0_conv_w3").reshape(MID, C)
    for v in ("norm1_w", "norm1_b", "norm2_w", "norm2_b", "proj_b", "fc1_b", "fc2_b", "cpb_b1"):
        arrays[v] = arr("L1_conv_" + v)
    for v in ("h_times", "pow_para", "ws_scalar", "ws_scalar2"):
        arrays[v] = arr("L1_conv_" + v).reshape(1)
    for v in ("qkv_w", "proj_w", "fc1_w", "fc2_w", "cpb_w1", "cpb_w2"):
        arrays[v + "T"] = np.ascontiguousarray(arr("L1_conv_" + v).T)
    arrays.update(shape_constants())

    nc = bacc.Bacc("TRN2", target_bir_lowering=False, num_devices=1)
    handles = {n: nc.dram_tensor("in_" + n, v.shape, mybir.dt.float32, kind="ExternalInput").ap()
               for n, v in arrays.items()}
    out = nc.dram_tensor("out_x", _OUT, mybir.dt.float32, kind="ExternalOutput").ap()
    program(nc, handles, out)
    r = run(nc, [{"in_" + n: v for n, v in arrays.items()}], core_ids=[0])
    return r.results[0]["out_x"]
```
